# Optimizing a Trainium2 kernel written in Bass

```python
import numpy as np
import jax
import jax.numpy as jnp

def _softmax(x, axis=-1):
    return jax.nn.softmax(x, axis=axis)

def _gelu(x):
    return jax.nn.gelu(x, approximate=True)

def _silu(x):
    return jax.nn.silu(x)

def _sigmoid(x):
    return jax.nn.sigmoid(x)

def _layernorm(x, axis=-1, eps=1e-05):
    m = jnp.mean(x, axis=axis, keepdims=True)
    v = jnp.var(x, axis=axis, keepdims=True)
    return (x - m) / jnp.sqrt(v + eps)

def _scatter_add(tgt, idx, src, axis=0):
    return tgt.at[idx].add(src)

def _segment_sum(src, seg, n):
    return jax.ops.segment_sum(src, seg, n)
kernel_name = 'mk_gps_d2_gnn_r8_24d7ae'

def setup_inputs(seed: int=0):
    np.random.seed(seed)
    _w = jnp.asarray

    def _rec_inputs():
        import jax
        import jax.numpy as jnp
        _gk = jax.random.key(seed)
        x = -0.000364 + 1 * jax.random.normal(jax.random.fold_in(_gk, 1), (1250, 768), jnp.float32)
        src = jax.random.randint(jax.random.fold_in(_gk, 2), (40000,), 0, 1250, jnp.int32)
        dst = jax.random.randint(jax.random.fold_in(_gk, 3), (40000,), 0, 1250, jnp.int32)
        _o = jnp.argsort(dst, stable=True)
        src = src[_o]
        dst = dst[_o]
        edge_weight = jax.random.uniform(jax.random.fold_in(_gk, 12), (40000,), jnp.float32, 0.0, 0.999998)
        return (x, src, dst, edge_weight)
    x, src, dst, edge_weight = _rec_inputs()

    def _L0_gnn_setup():
        import jax, jax.numpy as jnp
        import numpy as np
        N = 2500
        E_RAND = 40000
        NEG_SLOPE = 0.2

        def gat_layer(x, W, a_src, a_dst, bias, src, dst, heads, out_c, concat):
            n = x.shape[0]
            h = (x @ W).reshape(n, heads, out_c)
            al_s = jnp.einsum('nhc,hc->nh', h, a_src)
            al_d = jnp.einsum('nhc,hc->nh', h, a_dst)
            e = jax.nn.leaky_relu(al_s[src] + al_d[dst], NEG_SLOPE)
            m = jax.ops.segment_max(e, dst, num_segments=n)
            ex = jnp.exp(e - m[dst])
            z = jax.ops.segment_sum(ex, dst, num_segments=n)
            alpha = ex / (z[dst] + 1e-16)
            msg = h[src] * alpha[:, :, None]
            out = jax.ops.segment_sum(msg, dst, num_segments=n)
            out = out.reshape(n, heads * out_c) if concat else out.mean(axis=1)
            return out + bias
        key = jax.random.key(seed)
        ks = jax.random.split(key, 10)
        x = jax.random.normal(ks[0], (N, 768), dtype=jnp.float32)
        src = jax.random.randint(ks[1], (E_RAND,), 0, N)
        dst = jax.random.randint(ks[2], (E_RAND,), 0, N)
        loop = jnp.arange(N)
        edge_index = jnp.stack([jnp.concatenate([src, loop]), jnp.concatenate([dst, loop])])
        s = 1.0 / np.sqrt(768.0)
        W1 = jax.random.normal(ks[3], (768, 768), dtype=jnp.float32) * s
        a_src1 = jax.random.normal(ks[4], (8, 96), dtype=jnp.float32) * 0.1
        a_dst1 = jax.random.normal(ks[5], (8, 96), dtype=jnp.float32) * 0.1
        b1 = jnp.zeros((768,), dtype=jnp.float32)
        W2 = jax.random.normal(ks[6], (768, 768), dtype=jnp.float32) * s
        a_src2 = jax.random.normal(ks[7], (1, 768), dtype=jnp.float32) * 0.1
        a_dst2 = jax.random.normal(ks[8], (1, 768), dtype=jnp.float32) * 0.1
        b2 = jnp.zeros((768,), dtype=jnp.float32)
        return {'x': x, 'edge_index': edge_index, 'W1': W1, 'a_src1': a_src1, 'a_dst1': a_dst1, 'b1': b1, 'W2': W2, 'a_src2': a_src2, 'a_dst2': a_dst2, 'b2': b2}
    _L0_gnn_all = _L0_gnn_setup()
    _L0_gnn_in = {k: v for k, v in _L0_gnn_all.items() if k in ('W1', 'a_src1', 'a_dst1', 'b1', 'W2', 'a_src2', 'a_dst2', 'b2')}
    del _L0_gnn_all

    def _L0_mix_setup():
        import jax, jax.numpy as jnp
        import numpy as np
        EPS = 1e-06
        NUM_HEADS = 12

        def _phi(x):
            return jax.nn.elu(x) + 1.0
        key = jax.random.key(seed)
        k1, k2, k3, k4 = jax.random.split(key, 4)
        B, N, C = (4, 512, 768)
        x = jax.random.normal(k1, (B, N, C), dtype=jnp.float32)
        W_qkv = jax.random.normal(k2, (3 * C, C), dtype=jnp.float32) * (1.0 / np.sqrt(C))
        W_proj = jax.random.normal(k3, (C, C), dtype=jnp.float32) * (1.0 / np.sqrt(C))
        b_proj = jax.random.normal(k4, (C,), dtype=jnp.float32) * 0.01
        return {'x': x, 'W_qkv': W_qkv, 'W_proj': W_proj, 'b_proj': b_proj}
    _L0_mix_all = _L0_mix_setup()
    _L0_mix_in = {k: v for k, v in _L0_mix_all.items() if k in ('W_qkv', 'W_proj', 'b_proj')}
    del _L0_mix_all

    def _L0_ffn_setup():
        import jax, jax.numpy as jnp
        import numpy as np
        B, T, DM, DF, E, K = (4, 1024, 768, 384, 8, 2)
        key = jax.random.key(seed)
        k0, k1, k2, k3 = jax.random.split(key, 4)
        x = jax.random.normal(k0, (B, T, DM), jnp.float32)
        Wg = jax.random.normal(k1, (DM, E), jnp.float32) * 0.02
        W1 = jax.random.normal(k2, (E, DM, DF), jnp.float32) * 0.02
        b1 = jnp.zeros((E, DF), jnp.float32)
        W2 = jax.random.normal(k3, (E, DF, DM), jnp.float32) * 0.02
        b2 = jnp.zeros((E, DM), jnp.float32)
        return {'x': x, 'Wg': Wg, 'W1': W1, 'b1': b1, 'W2': W2, 'b2': b2}
    _L0_ffn_all = _L0_ffn_setup()
    _L0_ffn_in = {k: v for k, v in _L0_ffn_all.items() if k in ('Wg', 'W1', 'b1', 'W2', 'b2')}
    del _L0_ffn_all

    def _L1_gnn_setup():
        import jax, jax.numpy as jnp
        import numpy as np
        N = 6250
        E = 62500
        D = 768
        H = 256
        R = 32

        def _gcn(x, W, b, row, col, ew):
            x = x @ W
            n = x.shape[0]
            deg = jax.ops.segment_sum(ew, col, num_segments=n) + 1.0
            dinv = jax.lax.rsqrt(deg)
            norm = dinv[row] * ew * dinv[col]
            agg = jax.ops.segment_sum(norm[:, None] * x[row], col, num_segments=n)
            return agg + (dinv * dinv)[:, None] * x + b
        key = jax.random.key(seed)
        ks = jax.random.split(key, 8)
        d = D // R
        w = lambda k, sh: jax.random.normal(k, sh, jnp.float32) * 0.05
        return {'x': jax.random.normal(ks[0], (N, D), jnp.float32), 'edge_index': jax.random.randint(ks[1], (2, E), 0, N), 'edge_weight': jax.random.uniform(ks[2], (E,), jnp.float32), 'Wd': w(ks[3], (D, d)), 'bd': jnp.zeros((d,), jnp.float32), 'Wu': w(ks[4], (d, D)), 'bu': jnp.zeros((D,), jnp.float32), 'W1': w(ks[5], (D, H)), 'b1': jnp.zeros((H,), jnp.float32), 'W2': w(ks[6], (H, D)), 'b2': jnp.zeros((D,), jnp.float32)}
    _L1_gnn_all = _L1_gnn_setup()
    _L1_gnn_in = {k: v for k, v in _L1_gnn_all.items() if k in ('Wd', 'bd', 'Wu', 'bu', 'W1', 'b1', 'W2', 'b2')}
    del _L1_gnn_all

    def _L1_mix_setup():
        import jax, jax.numpy as jnp
        import numpy as np
        LN_EPS = 1e-05
        NORM_EPS = 1e-12

        def _layernorm(x, gamma, beta):
            mu = jnp.mean(x, axis=-1, keepdims=True)
            var = jnp.mean(jnp.square(x - mu), axis=-1, keepdims=True)
            return (x - mu) * jax.lax.rsqrt(var + LN_EPS) * gamma + beta

        def _l2norm(x):
            n = jnp.sqrt(jnp.sum(jnp.square(x), axis=-1, keepdims=True))
            return x / jnp.maximum(n, NORM_EPS)
        key = jax.random.key(seed)
        ks = jax.random.split(key, 4)
        B, N, C, E = (8, 512, 768, 768)
        x = jax.random.normal(ks[0], (B, N, C), dtype=jnp.float32)
        w_qkv = jax.random.normal(ks[1], (C, 3 * E), dtype=jnp.float32) * (1.0 / np.sqrt(C))
        w_proj = jax.random.normal(ks[2], (E, C), dtype=jnp.float32) * (1.0 / np.sqrt(E))
        ln_in_g = jnp.ones((C,), jnp.float32)
        ln_in_b = jnp.zeros((C,), jnp.float32)
        ln_out_g = jnp.ones((E,), jnp.float32)
        ln_out_b = jnp.zeros((E,), jnp.float32)
        return {'x': x, 'w_qkv': w_qkv, 'w_proj': w_proj, 'ln_in_g': ln_in_g, 'ln_in_b': ln_in_b, 'ln_out_g': ln_out_g, 'ln_out_b': ln_out_b}
    _L1_mix_all = _L1_mix_setup()
    _L1_mix_in = {k: v for k, v in _L1_mix_all.items() if k in ('w_qkv', 'w_proj', 'ln_in_g', 'ln_in_b', 'ln_out_g', 'ln_out_b')}
    del _L1_mix_all

    def _L1_ffn_setup():
        import jax, jax.numpy as jnp
        import numpy as np
        D_MODEL = 768
        KAN_HIDDEN = 256
        NUM_CP = 16
        DEGREE = 3
        RMIN, RMAX = (-4.0, 4.0)

        def bspline_basis(x, num_cp=NUM_CP, degree=DEGREE, rmin=RMIN, rmax=RMAX):
            h = (rmax - rmin) / (num_cp - degree)
            knots = rmin - degree * h + jnp.arange(num_cp + degree + 1, dtype=x.dtype) * h
            xe = x[..., None]
            b = ((xe >= knots[:-1]) & (xe < knots[1:])).astype(x.dtype)
            for d in range(1, degree + 1):
                t0 = knots[:-(d + 1)]
                t1 = knots[d:-1]
                t2 = knots[d + 1:]
                t3 = knots[1:-d]
                b = (xe - t0) / (t1 - t0) * b[..., :-1] + (t2 - xe) / (t2 - t3) * b[..., 1:]
            return b

        def kan_layer(x, w):
            basis = bspline_basis(x)
            return jnp.einsum('ndk,odk->no', basis, w)
        key = jax.random.key(seed)
        kx, k1, k2 = jax.random.split(key, 3)
        x = jax.random.normal(kx, (2, 256, D_MODEL), dtype=jnp.float32)
        w1 = jax.random.normal(k1, (KAN_HIDDEN, D_MODEL, NUM_CP), dtype=jnp.float32) * (1.0 / np.sqrt(D_MODEL * NUM_CP))
        w2 = jax.random.normal(k2, (D_MODEL, KAN_HIDDEN, NUM_CP), dtype=jnp.float32) * (1.0 / np.sqrt(KAN_HIDDEN * NUM_CP))
        return {'x': x, 'w1': w1, 'w2': w2}
    _L1_ffn_all = _L1_ffn_setup()
    _L1_ffn_in = {k: v for k, v in _L1_ffn_all.items() if k in ('w1', 'w2')}
    del _L1_ffn_all
    return {'x': x, 'src': src, 'dst': dst, 'edge_weight': edge_weight, 'L0_gnn_W1': _L0_gnn_in['W1'], 'L0_gnn_a_src1': _L0_gnn_in['a_src1'], 'L0_gnn_a_dst1': _L0_gnn_in['a_dst1'], 'L0_gnn_b1': _L0_gnn_in['b1'], 'L0_gnn_W2': _L0_gnn_in['W2'], 'L0_gnn_a_src2': _L0_gnn_in['a_src2'], 'L0_gnn_a_dst2': _L0_gnn_in['a_dst2'], 'L0_gnn_b2': _L0_gnn_in['b2'], 'L0_mix_W_qkv': _L0_mix_in['W_qkv'], 'L0_mix_W_proj': _L0_mix_in['W_proj'], 'L0_mix_b_proj': _L0_mix_in['b_proj'], 'L0_ffn_Wg': _L0_ffn_in['Wg'], 'L0_ffn_W1': _L0_ffn_in['W1'], 'L0_ffn_b1': _L0_ffn_in['b1'], 'L0_ffn_W2': _L0_ffn_in['W2'], 'L0_ffn_b2': _L0_ffn_in['b2'], 'L1_gnn_Wd': _L1_gnn_in['Wd'], 'L1_gnn_bd': _L1_gnn_in['bd'], 'L1_gnn_Wu': _L1_gnn_in['Wu'], 'L1_gnn_bu': _L1_gnn_in['bu'], 'L1_gnn_W1': _L1_gnn_in['W1'], 'L1_gnn_b1': _L1_gnn_in['b1'], 'L1_gnn_W2': _L1_gnn_in['W2'], 'L1_gnn_b2': _L1_gnn_in['b2'], 'L1_mix_w_qkv': _L1_mix_in['w_qkv'], 'L1_mix_w_proj': _L1_mix_in['w_proj'], 'L1_mix_ln_in_g': _L1_mix_in['ln_in_g'], 'L1_mix_ln_in_b': _L1_mix_in['ln_in_b'], 'L1_mix_ln_out_g': _L1_mix_in['ln_out_g'], 'L1_mix_ln_out_b': _L1_mix_in['ln_out_b'], 'L1_ffn_w1': _L1_ffn_in['w1'], 'L1_ffn_w2': _L1_ffn_in['w2']}

def reference(x, src, dst, edge_weight, L0_gnn_W1, L0_gnn_a_src1, L0_gnn_a_dst1, L0_gnn_b1, L0_gnn_W2, L0_gnn_a_src2, L0_gnn_a_dst2, L0_gnn_b2, L0_mix_W_qkv, L0_mix_W_proj, L0_mix_b_proj, L0_ffn_Wg, L0_ffn_W1, L0_ffn_b1, L0_ffn_W2, L0_ffn_b2, L1_gnn_Wd, L1_gnn_bd, L1_gnn_Wu, L1_gnn_bu, L1_gnn_W1, L1_gnn_b1, L1_gnn_W2, L1_gnn_b2, L1_mix_w_qkv, L1_mix_w_proj, L1_mix_ln_in_g, L1_mix_ln_in_b, L1_mix_ln_out_g, L1_mix_ln_out_b, L1_ffn_w1, L1_ffn_w2):
    import jax
    import jax.numpy as jnp

    def _L0_gnn_ref(x, edge_index, W1, a_src1, a_dst1, b1, W2, a_src2, a_dst2, b2):
        import jax, jax.numpy as jnp
        import numpy as np
        N = 2500
        E_RAND = 40000
        NEG_SLOPE = 0.2

        def gat_layer(x, W, a_src, a_dst, bias, src, dst, heads, out_c, concat):
            n = x.shape[0]
            h = (x @ W).reshape(n, heads, out_c)
            al_s = jnp.einsum('nhc,hc->nh', h, a_src)
            al_d = jnp.einsum('nhc,hc->nh', h, a_dst)
            e = jax.nn.leaky_relu(al_s[src] + al_d[dst], NEG_SLOPE)
            m = jax.ops.segment_max(e, dst, num_segments=n)
            ex = jnp.exp(e - m[dst])
            z = jax.ops.segment_sum(ex, dst, num_segments=n)
            alpha = ex / (z[dst] + 1e-16)
            msg = h[src] * alpha[:, :, None]
            out = jax.ops.segment_sum(msg, dst, num_segments=n)
            out = out.reshape(n, heads * out_c) if concat else out.mean(axis=1)
            return out + bias
        src, dst = (edge_index[0], edge_index[1])
        h = gat_layer(x, W1, a_src1, a_dst1, b1, src, dst, heads=8, out_c=96, concat=True)
        h = jax.nn.elu(h)
        out = gat_layer(h, W2, a_src2, a_dst2, b2, src, dst, heads=1, out_c=768, concat=False)
        return out

    def _L0_mix_ref(x, W_qkv, W_proj, b_proj):
        import jax, jax.numpy as jnp
        import numpy as np
        EPS = 1e-06
        NUM_HEADS = 12

        def _phi(x):
            return jax.nn.elu(x) + 1.0
        B, N, C = x.shape
        H = NUM_HEADS
        d = C // H
        qkv = (x @ W_qkv.T).reshape(B, N, 3, H, d)
        qkv = jnp.transpose(qkv, (2, 0, 3, 1, 4))
        q, k, v = (qkv[0], qkv[1], qkv[2])
        q = _phi(q)
        k = _phi(k)
        kv = jnp.einsum('bhnd,bhnm->bhmd', k, v)
        k_sum = k.sum(axis=-2)
        z = 1.0 / (jnp.einsum('bhnd,bhd->bhn', q, k_sum) + EPS)
        y = jnp.einsum('bhnd,bhmd,bhn->bhnm', q, kv, z)
        y = jnp.transpose(y, (0, 2, 1, 3)).reshape(B, N, C)
        return y @ W_proj.T + b_proj

    def _L0_ffn_ref(x, Wg, W1, b1, W2, b2):
        import jax, jax.numpy as jnp
        import numpy as np
        B, T, DM, DF, E, K = (4, 1024, 768, 384, 8, 2)
        m = x.shape[-1]
        xs = x.reshape(-1, m)
        S = xs.shape[0]
        n_exp = W1.shape[0]
        logits = xs @ Wg
        probs = jax.nn.softmax(logits, axis=-1)
        topv, topi = jax.lax.top_k(probs, K)
        cw = topv / jnp.sum(topv, axis=-1, keepdims=True)
        combine_weights = cw.T
        eid_flat = topi.T.reshape(-1)
        dispatch_mask = jnp.argsort(eid_flat)
        e_sorted = eid_flat[dispatch_mask]
        dispatched = xs[dispatch_mask % S]
        expert_outputs = jnp.zeros_like(dispatched)
        for e in range(n_exp):
            sel = (e_sorted == e)[:, None].astype(dispatched.dtype)
            h = jax.nn.relu(dispatched @ W1[e] + b1[e])
            expert_outputs = expert_outputs + sel * (h @ W2[e] + b2[e])
        rerouted = jnp.zeros((S * K, m), expert_outputs.dtype).at[dispatch_mask].set(expert_outputs)
        rerouted = rerouted.reshape(K, S, m)
        combined = jnp.einsum('ks,ksm->sm', combine_weights, rerouted)
        return combined.reshape(x.shape).astype(x.dtype)

    def _L1_gnn_ref(x, edge_index, edge_weight, Wd, bd, Wu, bu, W1, b1, W2, b2):
        import jax, jax.numpy as jnp
        import numpy as np
        N = 6250
        E = 62500
        D = 768
        H = 256
        R = 32

        def _gcn(x, W, b, row, col, ew):
            x = x @ W
            n = x.shape[0]
            deg = jax.ops.segment_sum(ew, col, num_segments=n) + 1.0
            dinv = jax.lax.rsqrt(deg)
            norm = dinv[row] * ew * dinv[col]
            agg = jax.ops.segment_sum(norm[:, None] * x[row], col, num_segments=n)
            return agg + (dinv * dinv)[:, None] * x + b
        h = jax.nn.relu(x @ Wd + bd) @ Wu + bu + x
        row, col = (edge_index[0], edge_index[1])
        h = jax.nn.relu(_gcn(h, W1, b1, row, col, edge_weight))
        h = _gcn(h, W2, b2, row, col, edge_weight)
        return h

    def _L1_mix_ref(x, w_qkv, w_proj, ln_in_g, ln_in_b, ln_out_g, ln_out_b):
        import jax, jax.numpy as jnp
        import numpy as np
        LN_EPS = 1e-05
        NORM_EPS = 1e-12

        def _layernorm(x, gamma, beta):
            mu = jnp.mean(x, axis=-1, keepdims=True)
            var = jnp.mean(jnp.square(x - mu), axis=-1, keepdims=True)
            return (x - mu) * jax.lax.rsqrt(var + LN_EPS) * gamma + beta

        def _l2norm(x):
            n = jnp.sqrt(jnp.sum(jnp.square(x), axis=-1, keepdims=True))
            return x / jnp.maximum(n, NORM_EPS)
        h = _layernorm(x, ln_in_g, ln_in_b)
        qkv = h @ w_qkv
        q, k, v = jnp.split(qkv, 3, axis=-1)
        phi_q = _l2norm(q)
        phi_k = _l2norm(k)
        kv = jnp.sum(phi_k * v, axis=1)
        attn = phi_q * kv[:, None, :]
        out = _layernorm(attn, ln_out_g, ln_out_b) @ w_proj
        return out

    def _L1_ffn_ref(x, w1, w2):
        import jax, jax.numpy as jnp
        import numpy as np
        D_MODEL = 768
        KAN_HIDDEN = 256
        NUM_CP = 16
        DEGREE = 3
        RMIN, RMAX = (-4.0, 4.0)

        def bspline_basis(x, num_cp=NUM_CP, degree=DEGREE, rmin=RMIN, rmax=RMAX):
            h = (rmax - rmin) / (num_cp - degree)
            knots = rmin - degree * h + jnp.arange(num_cp + degree + 1, dtype=x.dtype) * h
            xe = x[..., None]
            b = ((xe >= knots[:-1]) & (xe < knots[1:])).astype(x.dtype)
            for d in range(1, degree + 1):
                t0 = knots[:-(d + 1)]
                t1 = knots[d:-1]
                t2 = knots[d + 1:]
                t3 = knots[1:-d]
                b = (xe - t0) / (t1 - t0) * b[..., :-1] + (t2 - xe) / (t2 - t3) * b[..., 1:]
            return b

        def kan_layer(x, w):
            basis = bspline_basis(x)
            return jnp.einsum('ndk,odk->no', basis, w)
        B, T, D = x.shape
        input_dtype = x.dtype
        h = x.reshape(B * T, D).astype(jnp.float32)
        h = kan_layer(h, w1)
        h = kan_layer(h, w2)
        h = h.astype(input_dtype)
        return h.reshape(B, T, -1)
    edge_index = jnp.stack([src, dst])
    xn = _layernorm(x, axis=-1)
    x = x + _L0_gnn_ref(xn, edge_index, L0_gnn_W1, L0_gnn_a_src1, L0_gnn_a_dst1, L0_gnn_b1, L0_gnn_W2, L0_gnn_a_src2, L0_gnn_a_dst2, L0_gnn_b2) + _L0_mix_ref(xn[None], L0_mix_W_qkv, L0_mix_W_proj, L0_mix_b_proj)[0]
    x = x + _L0_ffn_ref(_layernorm(x, axis=-1)[None], L0_ffn_Wg, L0_ffn_W1, L0_ffn_b1, L0_ffn_W2, L0_ffn_b2)[0]
    xn = _layernorm(x, axis=-1)
    x = x + _L1_gnn_ref(xn, edge_index, edge_weight, L1_gnn_Wd, L1_gnn_bd, L1_gnn_Wu, L1_gnn_bu, L1_gnn_W1, L1_gnn_b1, L1_gnn_W2, L1_gnn_b2) + _L1_mix_ref(xn[None], L1_mix_w_qkv, L1_mix_w_proj, L1_mix_ln_in_g, L1_mix_ln_in_b, L1_mix_ln_out_g, L1_mix_ln_out_b)[0]
    x = x + _L1_ffn_ref(_layernorm(x, axis=-1)[None], L1_ffn_w1, L1_ffn_w2)[0]
    return x

_drawn_inputs = setup_inputs


def setup_inputs(seed=0):
    import zlib

    import numpy as np

    out = dict(_drawn_inputs(seed))
    spreads = {'L0_gnn_b1': (0.0, 0.1),
     'L0_gnn_b2': (0.0, 0.1),
     'L0_ffn_b1': (0.0, 0.271),
     'L0_ffn_b2': (0.0, 0.1),
     'L1_gnn_bd': (0.0, 0.8),
     'L1_gnn_bu': (0.0, 0.1),
     'L1_gnn_b1': (0.0, 0.1),
     'L1_gnn_b2': (0.0, 0.1),
     'L1_mix_ln_in_g': (1.0, 0.2),
     'L1_mix_ln_in_b': (0.0, 0.1),
     'L1_mix_ln_out_g': (1.0, 0.2),
     'L1_mix_ln_out_b': (0.0, 0.1)}
    factors = {'edge_weight': 3.684, 'L0_gnn_a_dst1': 3.176, 'L0_gnn_a_dst2': 4.322, 'L1_gnn_Wd': 4.146}
    for name, (base, spread) in spreads.items():
        noise = np.random.default_rng([zlib.crc32(name.encode()), seed]).standard_normal(out[name].shape)
        drawn = base * np.exp(spread * noise) if base else spread * noise
        out[name] = jnp.asarray(drawn.astype(out[name].dtype))
    for name, factor in factors.items():
        out[name] = (out[name] * factor).astype(out[name].dtype)
    return out
```

```python
from contextlib import ExitStack

import concourse.bass as bass
from concourse import mybir

ALU = mybir.AluOpType
ACT = mybir.ActivationFunctionType
AXX = mybir.AxisListType.X
F32 = mybir.dt.float32
I32 = mybir.dt.int32
BF16 = mybir.dt.bfloat16
FP16 = mybir.dt.float16

STAGE = 99

NODES, D, EDGES = 1250, 768, 40000
P = 128
TILE = 125
NT = NODES // TILE
KT = D // P
HALF = D // 2
HEADS, HC = 8, D // 8
FH, FD = 12, 64
EXP, DF = 8, 384
HID = 256
RANK = 24
NCP = 16
LN_EPS = 1e-5
SPAN = 0.2
SPLINE_H = 8.0 / 13.0
FAR = -1.0e30

COLS = [(0, 312), (624, 313)]

ET = -(-EDGES // P)
WIN = 32
NB = 40
NODES_P = WIN * NB
TB = EDGES * WIN // NODES // P
PRE = 4
SPREAD = 16
CHUNKS = -(-ET // SPREAD)
ECOLS = PRE + 3 * P
KINDS = 4
RING = 8
CREDIT = 32


def make_plan():
    packets, pieces, last = {}, {}, {}

    def packet(*key):
        packets[key] = len(packets)

    def piece(*key):
        pieces[key] = len(pieces)
        return key

    def used(*keys):
        for k in keys:
            last[k] = len(packets) - 1

    def transposes(s):
        for i in range(NT):
            packet("T", s, i)

    def token_major(name, w0, w1):
        a, b = piece(*w0), piece(*w1)
        for i in range(NT):
            packet(name, i)
        used(a, b)

    transposes("xn")
    token_major("mk", ("mWk", 0), ("mWk", 1))
    token_major("mv", ("mWv", 0), ("mWv", 1))
    packet("mP", 0)
    packet("mP", 1)
    for p in range(6):
        if p % 3 == 0:
            w = piece("mWq", p // 3)
        for n in range(2):
            packet("mq", p, n)
        if p % 3 == 2:
            used(w)
        for n in range(2):
            packet("my", p, n)
            packet("mz", p, n)
    token_major("mo", ("mWp", 0), ("mWp", 1))
    token_major("h1", ("gW1", 0), ("gW1", 1))
    for j in range(NT):
        for q in range(3):
            packet("neg", j, q)
    for h in range(HEADS):
        packet("srow", h, 0)
        packet("srow", h, 1)
    for h in range(HEADS + 1):
        if h < HEADS:
            for w in range(2):
                packet("drow", h, w, 0)
                packet("drow", h, w, 1)
        if h >= 1:
            packet("agg", h - 1)
    transposes("x2")
    token_major("h2", ("gW2", 0), ("gW2", 1))
    packet("srow2", 0)
    packet("srow2", 1)
    for w in range(2):
        packet("drow2", w, 0)
        packet("drow2", w, 1)
    for j in range(NT):
        packet("agg2", j)
    transposes("xf")
    packet("logit")
    packet("cwT", 0)
    packet("cwT", 1)
    for i in range(NT):
        packet("eb", i)
    for e in range(EXP):
        w = piece("eW1", e)
        for f in range(3):
            for n in range(2):
                packet("eh", e, f, n)
        used(w)
        w = piece("eW2", e)
        for i in range(NT):
            packet("eo", e, i)
        used(w)
    transposes("x3")
    packet("deg")
    for n in range(2):
        packet("ad", n)
    for k in range(KT):
        for n in range(2):
            packet("ah", k, n)
    w = piece("cW1")
    for i in range(NT):
        packet("cg", i)
    used(w)
    for j in range(NT):
        packet("ca", j)
    for f in range(2):
        for n in range(2):
            packet("cb", f, n)
    w = piece("cW2")
    for i in range(NT):
        packet("co", i)
    used(w)
    transposes("hin")
    token_major("vk", ("vWk", 0), ("vWk", 1))
    token_major("vv", ("vWv", 0), ("vWv", 1))
    packet("vkv")
    token_major("vq", ("vWq", 0), ("vWq", 1))
    transposes("at")
    token_major("vo", ("vWp", 0), ("vWp", 1))
    transposes("x4")
    for o in range(2):
        for n in range(2):
            packet("s1", o, n)
    for c in range(KT):
        for b in range(2):
            w = piece("kW1", c, b)
            used(w)
    for i in range(NT):
        packet("s2", i)
    return packets, pieces, last


def build(nc: bass.Bass, A, out):
    packets, pieces, last = make_plan()

    with ExitStack() as ctx:
        def sem(name):
            return ctx.enter_context(nc.semaphore(name))

        R_ACC, R_XT, R_CT, R_AA, R_H, R_WS = 7680, 7500, 7680, 12800, 7760, 7680
        arena = ctx.enter_context(nc.sbuf_tensor("arena", [P, R_ACC + R_XT + R_CT + R_AA + R_H + R_WS], F32))
        small = ctx.enter_context(nc.sbuf_tensor("small", [P, 2080], F32))
        ps = ctx.enter_context(nc.psum_tensor("ps", [P, 4, 1024], F32))

        def region(start, size):
            return arena[:, start:start + size]

        acc_r = region(0, R_ACC)
        xt_r = region(R_ACC, R_XT)
        ct_r = region(R_ACC + R_XT, R_CT)
        aa_r = region(R_ACC + R_XT + R_CT, R_AA)
        h_r = region(R_ACC + R_XT + R_CT + R_AA, R_H)
        ws_r = region(R_ACC + R_XT + R_CT + R_AA + R_H, R_WS)

        acc = acc_r.rearrange("p (t d) -> p t d", t=NT)[0:TILE]
        xT = xt_r[:, 0:KT * NODES].rearrange("p (k n) -> p k n", k=KT)
        H = h_r[0:TILE, 0:NT * D].rearrange("p (t d) -> p t d", t=NT)

        at = [0]

        def cut(n):
            at[0] += n
            assert at[0] <= 2080
            return small[:, at[0] - n:at[0]]

        ident = cut(128)
        ident16 = cut(64).bitcast(FP16)
        rowb = cut(768)
        st = cut(NT * 12)[0:TILE].rearrange("p (t c s) -> p t c s", t=NT, c=2)
        mv = cut(NT * 2)[0:TILE].rearrange("p (t s) -> p t s", t=NT)
        stdv = cut(NT)[0:TILE]
        rstd = cut(NT)[0:TILE]
        alS = cut(NT * 8)[0:TILE].rearrange("p (t h) -> p t h", t=NT)
        alD = cut(NT * 8)[0:TILE].rearrange("p (t h) -> p t h", t=NT)
        alS2 = cut(NT * 8)[0:TILE].rearrange("p (t h) -> p t h", t=NT)
        smax = cut(NT * 8)[0:TILE].rearrange("p (t h) -> p t h", t=NT)
        gD1 = cut(NT * 8)[0:TILE].rearrange("p (t h) -> p t h", t=NT)
        gD2 = cut(NT * 8)[0:TILE].rearrange("p (t h) -> p t h", t=NT)
        gz = cut(NT * 8)[0:TILE].rearrange("p (t h) -> p t h", t=NT)
        rz = cut(NT)[0:TILE]
        dinv = cut(NT)[0:TILE]
        rk = cut(NT)[0:TILE]
        rq = cut(NT)[0:TILE]
        flagf = cut(4)
        flagi = cut(2).bitcast(I32)
        eb1 = cut(EXP * 3).rearrange("p (e f) -> p e f", e=EXP)
        bu_c = cut(KT)
        bd_c = cut(1)
        gb_c = cut(4 * KT).rearrange("p (w k) -> p w k", w=4)
        centre = cut(NCP)
        onesc = cut(1)

        eo = [0]

        def ecut(n):
            eo[0] += n
            assert eo[0] <= R_XT
            return xt_r[:, eo[0] - n:eo[0]]

        iota_src = ecut(625).bitcast(FP16)
        src_c = ecut(ECOLS)
        dst_c = ecut(ECOLS)
        w_c = [ecut(ECOLS // 2).bitcast(BF16) for _ in range(3)]
        w_f = ecut(ECOLS)
        hi_row = ecut(ECOLS)
        viol = ecut(ECOLS)
        raw = ecut(9 * P).rearrange("p (a r e) -> p a r e", a=3, r=3)
        rawf = ecut(9 * P).rearrange("p (a r e) -> p a r e", a=3, r=3)
        iota_b = ecut(WIN)
        zero16 = ecut(256).bitcast(BF16)
        oh_src = h_r[:, 0:RING * 625].bitcast(FP16).rearrange("p (s n) -> p s n", s=RING)
        oh_dst = h_r[:, 5000:5000 + 2048].bitcast(BF16).rearrange("p (b t k w) -> p b t k w", b=2, t=SPREAD, k=KINDS)
        stage = ws_r[0:TILE, 0:2560].rearrange("p (b j k w) -> p b j k w", b=2, j=NT, k=KINDS)
        CT = ct_r[0:TILE, 0:6400].bitcast(FP16).rearrange("p (t n) -> p t n", t=NT)
        WA = aa_r[0:TILE, :].rearrange("p (t n) -> p t n", t=NT)

        mK = aa_r[0:TILE, 0:NT * D].rearrange("p (t d) -> p t d", t=NT)
        yT = aa_r[:, 0:KT * NODES].rearrange("p (k n) -> p k n", k=KT)
        qT = aa_r[:, 7680:7680 + 2500].rearrange("p (b n) -> p b n", b=2)
        tE = aa_r[:, 10180:10180 + 1536].rearrange("p (b n) -> p b n", b=2)
        Pbd = aa_r[:, 11716:11716 + 768].rearrange("p (k m) -> p k m", k=KT)
        Kbd = ws_r[:, 6912:6912 + 768].rearrange("p (k m) -> p k m", k=KT)
        AT = aa_r[0:TILE, 0:NT * NODES].rearrange("p (t n) -> p t n", t=NT)
        H97 = h_r[0:TILE, 0:NT * HEADS * (HC + 1)].rearrange("p (t h c) -> p t h c", t=NT, h=HEADS)
        H769 = h_r[0:TILE, 0:NT * (D + 1)].rearrange("p (t c) -> p t c", t=NT)
        negA = aa_r[0:TILE, 0:6250].bitcast(BF16).rearrange("p (t n) -> p t n", t=NT)
        negX = xt_r[0:TILE, 0:6250].bitcast(BF16).rearrange("p (t n) -> p t n", t=NT)
        dummy = aa_r[0:TILE, 6300:6300 + 625].bitcast(BF16)
        arow = aa_r[0:TILE, 7000:7000 + 2 * D].rearrange("p (w d) -> p w d", w=2)
        prod = aa_r[0:TILE, 8560:8560 + 2 * D].rearrange("p (w d) -> p w d", w=2)
        srow = aa_r[0:TILE, 10200:10200 + 2500].rearrange("p (b n) -> p b n", b=2)
        drow = xt_r[0:TILE, 0:5000].rearrange("p (b w n) -> p b w n", b=2, w=2)
        e2 = xt_r[0:TILE, 5000:7500].rearrange("p (b n) -> p b n", b=2)
        O = ws_r[0:TILE, 0:NT * D].rearrange("p (t d) -> p t d", t=NT)
        hT = aa_r[:, 0:7500].rearrange("p (b f n) -> p b f n", b=2, f=3)
        wg = aa_r[:, 7600:7648].rearrange("p (k e) -> p k e", k=KT)
        pr = aa_r[0:TILE, 7700:7780].rearrange("p (t e) -> p t e", t=NT)
        rank = aa_r[0:TILE, 7780:7860].rearrange("p (t e) -> p t e", t=NT)
        cmpb = aa_r[0:TILE, 7860:7940].rearrange("p (t e) -> p t e", t=NT)
        cw = aa_r[0:TILE, 7940:8020].rearrange("p (t e) -> p t e", t=NT)
        rsum = aa_r[0:TILE, 8020:8030]
        cwT = aa_r[0:EXP, 8100:8100 + NODES]
        eb2 = aa_r[0:EXP, 9400:9400 + D]
        haT = ct_r[:, 0:KT * NODES].rearrange("p (k n) -> p k n", k=KT)
        uT = ws_r[0:RANK, 6000:6000 + NODES]
        wu = ws_r[0:RANK, 5000:5000 + D]
        wd = ws_r[:, 4700:4700 + KT * RANK].rearrange("p (k r) -> p k r", k=KT)
        G1 = xt_r[0:TILE, 0:NT * HID].rearrange("p (t c) -> p t c", t=NT)
        G2 = xt_r[0:TILE, 2560:2560 + NT * HID].rearrange("p (t c) -> p t c", t=NT)
        agT = ct_r[:, 2560:2560 + 2 * NODES].rearrange("p (k n) -> p k n", k=2)
        gtmp = ct_r[0:TILE, 0:NT * HID].rearrange("p (t c) -> p t c", t=NT)
        hin = aa_r[0:TILE, 0:NT * D].rearrange("p (t d) -> p t d", t=NT)
        vK = aa_r[0:TILE, 0:NT * D].rearrange("p (t d) -> p t d", t=NT)
        sq = ct_r[0:TILE, 0:D]
        kvrow = ct_r[0:TILE, D:2 * D]
        t1 = [h_r[:, 1250 * n:1250 * n + 1250] for n in range(2)]
        kns = [h_r[:, 1250 * n:1250 * n + 1250] for n in (2, 3)]
        kb = [h_r[:, 1250 * n:1250 * n + 1250] for n in (4, 5)] + [ct_r[:, 0:1250]]
        kq2 = [ct_r[:, 1250 * n:1250 * n + 1250] for n in (1, 2)]
        h1T = ct_r[:, 5000:7500].rearrange("p (k n) -> p k n", k=2)
        w2v = arena[:, R_ACC + R_XT + R_CT:R_ACC + R_XT + R_CT + 32 * D].rearrange("p (k d) -> p k d", k=32)
        b2a, b2ns, b2s2 = (xt_r[:, 2000 * n:2000 * n + 2000] for n in range(3))
        bb = [ct_r[:, 2000 * n:2000 * n + 2000] for n in range(2)]

        wslot = [ws_r[:, 2304 * n:2304 * n + 2304] for n in range(3)]

        packet_ready = sem("packet_ready")
        slot_free = [sem(f"slot_free{n}") for n in range(4)]
        piece_in = [sem(f"piece_in{n}") for n in range(3)]
        act_step = sem("act_step")
        dve_step = sem("dve_step")
        pool_step = sem("pool_step")
        events = {}

        def ev(name):
            if name not in events:
                events[name] = sem("ev_" + name)
            return events[name]

        def slot(g):
            return ps[:, g % 4, :]

        def banks(g, w):
            return slot(g).rearrange("p (b n) -> p b n", b=2)[:, :, 0:w]

        class Tally:

            def __init__(self, engine, semaphore):
                self.engine, self.semaphore, self.n = engine, semaphore, 0

            def step(self, ins):
                ins.then_inc(self.semaphore, 1)
                self.n += 1
                return ins

            def settle(self):
                self.engine.wait_ge(self.semaphore, self.n)

        def take(engine, *key):
            g = packets[key]
            engine.wait_ge(packet_ready, g + 1)
            return g

        def give(ins, g):
            ins.then_inc(slot_free[g % 4], 1)

        def gone(engine, *key):
            g = packets[key]
            for q in range(max(0, g - 3), g + 1):
                engine.wait_ge(slot_free[q % 4], q // 4 + 1)

        def emptied(engine, *key):
            g = packets[key]
            engine.wait_ge(slot_free[g % 4], g // 4 + 1)

        block = ctx.enter_context(nc.Block())

        @block.sync
        def _(sp):
            def load(dst, src, name):
                sp.dma_start(dst, src, allow_slow_non_contiguous=(name == "cols")).then_inc(ev(name), 16)

            sp.wait_ge(ev("raw_filled"), 1)
            for a, t in enumerate((A["src"], A["dst"], A["edge_weight"])):
                t = t.bitcast(F32) if a < 2 else t
                full = t[0:2 * P * P].rearrange("(r p e) -> p r e", r=2, p=P)
                load(raw[:, a, 0:2, :], full, "edges")
                load(raw[0:56, a, 2, :], t[2 * P * P:312 * P].rearrange("(p e) -> p e", p=56), "edges")
                load(raw[56:57, a, 2, 0:64], t[312 * P:EDGES].rearrange("(p e) -> p e", p=1), "edges")
            load(acc, A["x"].rearrange("(t p) d -> p t d", p=TILE), "x")
            load(eb1, A["L0_ffn_b1"].rearrange("e (f p) -> p e f", p=P), "cols")
            load(bu_c, A["L1_gnn_bu"].rearrange("(k p) -> p k", p=P), "cols")
            load(bd_c[0:RANK], A["L1_gnn_bd"].rearrange("(k p) -> p k", p=RANK), "cols")
            for w, n in enumerate(("in_g", "in_b", "out_g", "out_b")):
                load(gb_c[:, w, :], A["L1_mix_ln_" + n].rearrange("(k p) -> p k", p=P), "cols")
            load(rowb[0:TILE], A["L0_mix_b_proj"].partition_broadcast(TILE), "rowb")

            def square(t, lo):
                return t[:, lo:lo + HALF].rearrange("(k p) n -> p k n", p=P)

            WT = {"mWk": (A["mixT"], D), "mWv": (A["mixT"], 2 * D), "mWq": (A["mixT"], 0), "mWp": (A["projT"], 0),
                  "gW1": (A["L0_gnn_W1"], 0), "gW2": (A["L0_gnn_W2"], 0),
                  "vWq": (A["L1_mix_w_qkv"], 0), "vWk": (A["L1_mix_w_qkv"], D), "vWv": (A["L1_mix_w_qkv"], 2 * D),
                  "vWp": (A["L1_mix_w_proj"], 0)}
            order = sorted(pieces, key=pieces.get)

            def send(key):
                n = pieces[key]
                if n >= 3:
                    sp.wait_ge(packet_ready, last[order[n - 3]] + 1)
                name = key[0]
                if name in WT:
                    t, lo = WT[name]
                    dst, src = wslot[n % 3].rearrange("p (k n) -> p k n", k=KT), square(t, lo + HALF * key[1])
                elif name == "eW1":
                    dst, src = wslot[n % 3].rearrange("p (k n) -> p k n", k=KT), square(A["L0_ffn_W1"][key[1]], 0)
                elif name == "eW2":
                    dst = wslot[n % 3].rearrange("p (k n) -> p k n", k=3)
                    src = A["L0_ffn_W2"][key[1]].rearrange("(k p) n -> p k n", p=P)
                elif name == "cW1":
                    dst = wslot[n % 3][:, 0:KT * HID].rearrange("p (k n) -> p k n", k=KT)
                    src = A["L1_gnn_W1"].rearrange("(k p) n -> p k n", p=P)
                elif name == "cW2":
                    dst = wslot[n % 3][:, 0:2 * D].rearrange("p (k n) -> p k n", k=2)
                    src = A["L1_gnn_W2"].rearrange("(k p) n -> p k n", p=P)
                sp.dma_start(dst, src).then_inc(piece_in[n % 3], 16)

            sp.wait_ge(ev("adj_all"), 1)
            sp.dma_start(A["spill_w"], WA).then_inc(ev("spill"), 16)
            for key in order[0:8]:
                send(key)
            sp.wait_ge(ev("rowb_used"), 1)
            load(rowb[0:TILE], A["L0_gnn_b2"].partition_broadcast(TILE), "rowb")
            sp.wait_ge(ev("mo_done"), 1)
            load(arow[:, 0, :], A["L0_gnn_a_src1"].rearrange("h c -> (h c)").partition_broadcast(TILE), "arow")
            load(arow[:, 1, :], A["L0_gnn_a_dst1"].rearrange("h c -> (h c)").partition_broadcast(TILE), "arow")
            for key in order[8:10]:
                send(key)
            sp.wait_ge(ev("rowb_used"), 2)
            load(rowb[0:TILE], A["L0_gnn_b1"].partition_broadcast(TILE), "rowb")
            sp.wait_ge(ev("neg_done"), 1)
            sp.dma_start(A["spill_n"], negA).then_inc(ev("spill"), 16)
            sp.wait_ge(packet_ready, packets["T", "x2", NT - 1] + 1)
            for key in order[10:12]:
                send(key)
            load(arow[:, 0, :], A["L0_gnn_a_src2"].rearrange("h c -> (h c)").partition_broadcast(TILE), "arow")
            load(arow[:, 1, :], A["L0_gnn_a_dst2"].rearrange("h c -> (h c)").partition_broadcast(TILE), "arow")
            sp.wait_ge(packet_ready, packets["h2", NT - 1] + 1)
            sp.wait_ge(ev("spill"), 32)
            load(negX, A["spill_n"], "neg_back")
            sp.wait_ge(packet_ready, packets["agg2", NT - 1] + 1)
            load(wg, A["L0_ffn_Wg"].rearrange("(k p) e -> p k e", p=P), "wg")
            load(eb2, A["L0_ffn_b2"], "wg")
            ffn = [k for k in order if k[0] in ("eW1", "eW2")]
            for key in ffn:
                send(key)
            sp.wait_ge(packet_ready, packets["eo", EXP - 1, NT - 1] + 1)
            load(wd, A["L1_gnn_Wd"].rearrange("(k p) r -> p k r", p=P), "wd")
            load(wu, A["L1_gnn_Wu"], "wd")
            gone(sp, "eo", EXP - 1, NT - 1)
            load(WA, A["spill_w"], "wa_back")
            sp.wait_ge(ev("rowb_used"), 3)
            load(rowb[0:TILE, 0:HID], A["L1_gnn_b1"].partition_broadcast(TILE), "rowb")
            sp.wait_ge(packet_ready, packets["ah", KT - 1, 1] + 1)
            for key in (("cW1",), ("cW2",)):
                send(key)
            sp.wait_ge(ev("rowb_used"), 4)
            load(rowb[0:TILE], A["L1_gnn_b2"].partition_broadcast(TILE), "rowb")
            for key in order:
                if key[0] in ("vWk", "vWv", "vWq", "vWp"):
                    send(key)
            for key in order:
                if key[0] == "kW1":
                    n = pieces[key]
                    if n >= 3:
                        if order[n - 3][0] == "kW1":
                            c, b = order[n - 3][1:]
                            sp.wait_ge(ev("s1_mm"), c * NCP + b * 8 + 8)
                        else:
                            sp.wait_ge(packet_ready, last[order[n - 3]] + 1)
                    c, b = key[1:]
                    sp.dma_start(wslot[n % 3][:, 0:8 * HID].rearrange("p (j o) -> p j o", j=8),
                                 A["kw1"][8 * b:8 * b + 8, c * P:c * P + P, :].rearrange("j d o -> d j o"))\
                        .then_inc(piece_in[n % 3], 16)
                    if key == ("kW1", 0, 0):
                        sp.wait_ge(packet_ready, packets["T", "x4", NT - 1] + 1)
                        load(w2v[:, 0:16, :], A["kw2"][:, 0:P, :].rearrange("j d o -> d j o"), "kw2")
            sp.wait_ge(packet_ready, packets["s1", 1, 1] + 1)
            load(w2v[:, 16:32, :], A["kw2"][:, P:2 * P, :].rearrange("j d o -> d j o"), "kw2")
            outv = out.rearrange("(t p) d -> p t d", p=TILE)
            for i in range(NT):
                sp.wait_ge(ev("final"), i + 1)
                sp.dma_start(outv[:, i, :], acc[:, i, :]).then_inc(ev("out"), 16)
            sp.wait_ge(ev("out"), 16 * NT)

        @block.gpsimd
        def _(pool):
            own = Tally(pool, pool_step)
            own.step(pool.memset(raw[:, 0:2, :, :].bitcast(I32), -1))
            own.step(pool.memset(raw[:, 2, :, :], 0.0))
            own.step(pool.memset(ident, 0.0))
            own.settle()
            pool.memset(onesc, 1.0).then_inc(ev("raw_filled"), 1)
            own.step(pool.affine_select(out=ident, in_=ident, compare_op=ALU.not_equal, fill=1.0, base=0,
                                        pattern=[[-1, P]], channel_multiplier=1))
            own.settle()
            own.step(pool.tensor_copy(ident16, ident))
            own.step(pool.iota(iota_src, [[1, NODES]], base=0, channel_multiplier=0,
                               allow_small_or_imprecise_dtypes=True))
            own.step(pool.iota(iota_b, [[1, WIN]], base=0, channel_multiplier=0,
                               allow_small_or_imprecise_dtypes=True))
            own.step(pool.iota(hi_row[:, 0:376], [[WIN, 47], [0, 8]], base=WIN, channel_multiplier=0,
                               allow_small_or_imprecise_dtypes=True))
            own.step(pool.iota(centre, [[-2, NCP]], base=15, channel_multiplier=0,
                               allow_small_or_imprecise_dtypes=True))
            own.step(pool.memset(zero16, 0.0))
            own.settle()
            pool.tensor_scalar(centre, centre, 0.5, 0.0, ALU.mult, ALU.add).then_inc(ev("consts"), 1)

            pool.sem_inc(ev("staged"), 2)
            pool.sem_inc(ev("unstaged"), 2)
            pool.sem_inc(ev("next_block"), 1)
            pool.sem_inc(ev("tiles_done"), CREDIT)

            flag = None
            pool.wait_ge(ev("flag"), 1)
            flag = pool.value_load(flagi[0:1, 0:1], min_val=0, max_val=EDGES)

            def unstage(b, par, done):
                c = bass.ds(b * WIN, WIN)
                pool.wait_ge(ev("staged"), done + 3)
                k = stage[:, par]
                pool.tensor_copy(CT[:, :, c], k[:, :, 0, :]).then_inc(ev("unst_a"), 1)
                pool.tensor_tensor(k[:, :, 3, :], k[:, :, 3, :], k[:, :, 2, :], ALU.add).then_inc(ev("unst_b"), 1)
                pool.wait_ge(ev("unst_b"), done + 1)
                pool.wait_ge(ev("unst_a"), done + 1)
                pool.tensor_tensor(WA[:, :, c], k[:, :, 3, :], k[:, :, 1, :], ALU.add).then_inc(ev("unstaged"), 1)

            with pool.Fori(0, NB // 2) as bp:
                for par in range(2):
                    unstage(bp * 2 + par, par, bp * 2 + par)
            pool.wait_ge(ev("unstaged"), NB + 2)
            for i in range(NT):
                own.step(pool.tensor_tensor(WA[:, i, i * TILE:i * TILE + TILE], WA[:, i, i * TILE:i * TILE + TILE],
                                            ident[0:TILE, 0:TILE], ALU.add))
            own.settle()
            pool.memset(flagf[0:1, 2:3], 0.0).then_inc(ev("adj_all"), 1)

        @block.tensor
        def _(pe):
            def take_slot(*key):
                g = packets[key]
                if g >= 4:
                    pe.wait_ge(slot_free[g % 4], g // 4)
                return g

            def ready(ins):
                ins.then_inc(packet_ready, 1)

            def weights(*key):
                n = pieces[key]
                pe.wait_ge(piece_in[n % 3], 16 * (n // 3 + 1))
                return wslot[n % 3]

            pe.wait_ge(ev("consts"), 1)
            pe.wait_ge(ev("edges_f"), 1)
            for a in range(3):
                for r in range(3):
                    last_mm = pe.transpose(ps[:, a, r * P:r * P + P], rawf[:, a, r, :], ident)
                last_mm.then_inc(ev("edges_t"), 1)
            pe.wait_ge(ev("viol"), 1)
            pe.matmul(ps[0:1, 3, 0:1], flagf[:, 0:1], onesc, start=True, stop=True).then_inc(ev("flag_sum"), 1)
            pe.wait_ge(ev("flag"), 1)
            flag = pe.value_load(flagi[0:1, 0:1], min_val=0, max_val=EDGES)

            def edge_tiles(par, tile0):
                for u in range(SPREAD):
                    pe.wait_ge(ev("src_hot"), tile0 + (u + 1))
                    s = u % RING
                    for j in range(NT):
                        bank = 2 * (2 * par + j // 8) + (j % 8) // 4
                        o = ps[0:TILE, 2 * par + j // 8, (j % 8) * P:(j % 8) * P + P]
                        mm = pe.matmul(o, oh_src[:, s, j * TILE:j * TILE + TILE], oh_dst[:, par, u, :, :],
                                       start=False, stop=False, skip_group_check=True)
                    mm.then_inc(ev("tiles_done"), 1)

            def open_block(par, b):
                pe.wait_ge(ev("staged"), b + 1)
                for q in range(3):
                    pe.matmul(ps[0:TILE, 2 * par + q // 2, 512 * (q % 2):512 * (q % 2) + (512 if q < 2 else 256)],
                              zero16[:, 0:TILE], zero16[:, 0:512 if q < 2 else 256], start=True, stop=False,
                              skip_group_check=True)

            with pe.If(flag == 0):
                with pe.Fori(0, NB // 2) as bp:
                    for par in range(2):
                        b = bp * 2 + par
                        open_block(par, b)
                        pe.wait_ge(ev("dst_hot"), b + 1)
                        edge_tiles(par, b * SPREAD)
            with pe.Else():
                with pe.Fori(0, NB // 2) as bp:
                    for par in range(2):
                        b = bp * 2 + par
                        open_block(par, b)
                        with pe.Fori(0, CHUNKS) as ch:
                            n = b * CHUNKS + ch
                            pe.wait_ge(ev("dst_hot"), n + 1)
                            edge_tiles(par, n * SPREAD)
            pe.wait_ge(ev("staged"), NB + 2)
            pe.wait_ge(ev("adj_all"), 1)

            def transposes(s, src, event):
                for i in range(NT):
                    pe.wait_ge(ev(event), i + 1)
                    g = take_slot("T", s, i)
                    for k in range(KT):
                        o = slot(g)[:, 512 * (k // 3) + TILE * (k % 3):512 * (k // 3) + TILE * (k % 3) + TILE]
                        mm = pe.transpose(o, src[:, i, k * P:k * P + P], ident[0:TILE, 0:TILE])
                    ready(mm)

            def token_major(name, xt, w0, w1, kt=KT, cols=HALF):
                a, b = weights(*w0), weights(*w1)
                for i in range(NT):
                    g = take_slot(name, i)
                    for half, w in enumerate((a, b)):
                        w = w.rearrange("p (k n) -> p k n", k=KT)
                        for k in range(KT):
                            mm = pe.matmul(slot(g)[0:TILE, 512 * half:512 * half + HALF],
                                           xt[:, k, i * TILE:i * TILE + TILE], w[:, k, :],
                                           start=(k == 0), stop=(k == KT - 1))
                    ready(mm)

            def columns(g, n, rows, terms):
                lo, w = COLS[n]
                for b in range(2):
                    for t, (stat, mov) in enumerate(terms):
                        mm = pe.matmul(slot(g)[0:rows, 512 * b:512 * b + w], stat,
                                       mov[:, lo + b * w:lo + b * w + w],
                                       start=(t == 0), stop=(t == len(terms) - 1))
                return mm

            def broadcast_row(keys, col):
                for part, key in enumerate(keys):
                    g = take_slot(*key)
                    for q, i in enumerate(range(8) if part == 0 else (8, 9)):
                        mm = pe.matmul(slot(g)[0:TILE, 512 * (q // 4) + TILE * (q % 4):512 * (q // 4) + TILE * (q % 4) + TILE],
                                       col(i).broadcast_to([TILE, TILE]), ident[0:TILE, 0:TILE],
                                       start=True, stop=True)
                    ready(mm)

            transposes("xn", H, "ln_xn")
            gone(pe, "T", "xn", NT - 1)
            token_major("mk", xT, ("mWk", 0), ("mWk", 1))
            token_major("mv", xT, ("mWv", 0), ("mWv", 1))
            gone(pe, "mk", NT - 1)
            gone(pe, "mv", NT - 1)
            for q in range(2):
                g = take_slot("mP", q)
                for p in range(4 * q, min(4 * q + 4, KT)):
                    o = 256 * (p % 4)
                    for i in range(NT):
                        pe.matmul(slot(g)[:, o:o + P], mK[:, i, p * P:p * P + P], H[:, i, p * P:p * P + P],
                                  start=(i == 0), stop=(i == NT - 1))
                    for i in range(NT):
                        mm = pe.matmul(slot(g)[:, o + P:o + 2 * P], mK[:, i, p * P:p * P + P],
                                       onesc[0:TILE].broadcast_to([TILE, P]), start=(i == 0), stop=(i == NT - 1))
                ready(mm)
            pe.wait_ge(ev("P_in"), 1)
            for p in range(KT):
                w = weights("mWq", p // 3).rearrange("p (k n) -> p k n", k=KT)
                for n in range(2):
                    g = take_slot("mq", p, n)
                    ready(columns(g, n, P, [(w[:, k, (p % 3) * P:(p % 3) * P + P], xT[:, k, :]) for k in range(KT)]))
                for n in range(2):
                    if n == 0:
                        gone(pe, "mq", p, 1)
                    g = take_slot("my", p, n)
                    ready(columns(g, n, P, [(Pbd[:, p, :], qT[:, p % 2, :])]))
                    g = take_slot("mz", p, n)
                    ready(columns(g, n, P, [(Kbd[:, p, :], qT[:, p % 2, :])]))
            gone(pe, "mz", KT - 1, 1)
            token_major("mo", yT, ("mWp", 0), ("mWp", 1))

            token_major("h1", xT, ("gW1", 0), ("gW1", 1))
            for j in range(NT):
                for q in range(3):
                    g = take_slot("neg", j, q)
                    n = 4 if q < 2 else 2
                    o16 = slot(g)[0:TILE, 0:252].bitcast(FP16)
                    for i in range(n):
                        mm = pe.transpose(o16[:, i * 126:i * 126 + TILE],
                                          CT[:, 4 * q + i, j * TILE:j * TILE + TILE], ident16[0:TILE, 0:TILE])
                    ready(mm)
            pe.wait_ge(ev("al"), 1)
            for h in range(HEADS):
                broadcast_row([("srow", h, 0), ("srow", h, 1)], lambda i: alS[:, i, h:h + 1])
            pe.wait_ge(ev("gD"), 1)
            for h in range(-1, HEADS):
                n = h + 1
                if n < HEADS:
                    broadcast_row([("drow", n, 0, 0), ("drow", n, 0, 1)], lambda i: gD1[:, i, n:n + 1])
                    broadcast_row([("drow", n, 1, 0), ("drow", n, 1, 1)], lambda i: gD2[:, i, n:n + 1])
                if h < 0:
                    continue
                g = take_slot("agg", h)
                for i in range(NT):
                    pe.wait_ge(ev("A_in"), h * NT + i + 1)
                    for j in range(NT):
                        mm = pe.matmul(slot(g)[0:TILE, 512 * (j // 5) + 97 * (j % 5):512 * (j // 5) + 97 * (j % 5) + 97],
                                       AT[:, i, j * TILE:j * TILE + TILE], H97[:, i, h, :],
                                       start=(i == 0 and j % 5 == 0), stop=(i == NT - 1), skip_group_check=True)
                    if i < NT - 1:
                        mm.then_inc(ev("A_used"), 1)
                ready(mm)

            transposes("x2", O, "ln_x2")
            gone(pe, "T", "x2", NT - 1)
            token_major("h2", xT, ("gW2", 0), ("gW2", 1))
            pe.wait_ge(ev("al"), 2)
            broadcast_row([("srow2", 0), ("srow2", 1)], lambda i: alS[:, i, 0:1])
            pe.wait_ge(ev("gD"), 2)
            broadcast_row([("drow2", 0, 0), ("drow2", 0, 1)], lambda i: gD1[:, i, 0:1])
            broadcast_row([("drow2", 1, 0), ("drow2", 1, 1)], lambda i: gD2[:, i, 0:1])
            pe.wait_ge(ev("A_in"), HEADS * NT + NT)
            for j in range(NT):
                g = take_slot("agg2", j)
                for b, (lo, w) in enumerate(((0, 385), (385, 384))):
                    for i in range(NT):
                        mm = pe.matmul(slot(g)[0:TILE, 512 * b:512 * b + w], AT[:, i, j * TILE:j * TILE + TILE],
                                       H769[:, i, lo:lo + w], start=(i == 0), stop=(i == NT - 1))
                ready(mm)

            transposes("xf", H, "ln_xf")
            gone(pe, "T", "xf", NT - 1)
            pe.wait_ge(ev("wg"), 32)
            g = take_slot("logit")
            for i in range(NT):
                for k in range(KT):
                    mm = pe.matmul(slot(g)[0:TILE, 8 * i:8 * i + 8], xT[:, k, i * TILE:i * TILE + TILE], wg[:, k, :],
                                   start=(k == 0), stop=(k == KT - 1))
            ready(mm)
            pe.wait_ge(ev("cw"), 1)
            for n in range(2):
                g = take_slot("cwT", n)
                for i in range(5):
                    mm = pe.transpose(slot(g)[0:EXP, 512 * (i // 4) + TILE * (i % 4):512 * (i // 4) + TILE * (i % 4) + TILE],
                                      cw[:, 5 * n + i, :], ident[0:TILE, 0:TILE])
                ready(mm)
            gone(pe, "cwT", 1)
            for i in range(NT):
                g = take_slot("eb", i)
                for b in range(2):
                    mm = pe.matmul(slot(g)[0:TILE, 512 * b:512 * b + HALF], cwT[:, i * TILE:i * TILE + TILE],
                                   eb2[:, b * HALF:b * HALF + HALF], start=True, stop=True)
                ready(mm)
            for e in range(EXP):
                w = weights("eW1", e).rearrange("p (k n) -> p k n", k=KT)
                for f in range(3):
                    for n in range(2):
                        g = take_slot("eh", e, f, n)
                        ready(columns(g, n, P, [(w[:, k, f * P:f * P + P], xT[:, k, :]) for k in range(KT)]))
                w = weights("eW2", e).rearrange("p (k n) -> p k n", k=3)
                gone(pe, "eh", e, 2, 1)
                for i in range(NT):
                    g = take_slot("eo", e, i)
                    for b in range(2):
                        for f in range(3):
                            mm = pe.matmul(slot(g)[0:TILE, 512 * b:512 * b + HALF],
                                           hT[:, e % 2, f, i * TILE:i * TILE + TILE],
                                           w[:, f, b * HALF:b * HALF + HALF], start=(f == 0), stop=(f == 2))
                    ready(mm)

            transposes("x3", H, "ln_x3")
            gone(pe, "T", "x3", NT - 1)
            pe.wait_ge(ev("wa_back"), 16)
            g = take_slot("deg")
            for j in range(NT):
                for i in range(NT):
                    mm = pe.matmul(slot(g)[0:TILE, j:j + 1], WA[:, i, j * TILE:j * TILE + TILE], onesc[0:TILE],
                                   start=(i == 0), stop=(i == NT - 1))
            ready(mm)
            pe.wait_ge(ev("wd"), 32)
            for n in range(2):
                g = take_slot("ad", n)
                ready(columns(g, n, RANK, [(wd[:, k, :], xT[:, k, :]) for k in range(KT)]))
            gone(pe, "ad", 1)
            for k in range(KT):
                for n in range(2):
                    g = take_slot("ah", k, n)
                    ready(columns(g, n, P, [(wu[:, k * P:k * P + P], uT)]))
            w = weights("cW1")[:, 0:KT * HID].rearrange("p (k n) -> p k n", k=KT)
            gone(pe, "ah", KT - 1, 1)
            for i in range(NT):
                g = take_slot("cg", i)
                for k in range(KT):
                    mm = pe.matmul(slot(g)[0:TILE, 0:HID], haT[:, k, i * TILE:i * TILE + TILE], w[:, k, :],
                                   start=(k == 0), stop=(k == KT - 1))
                ready(mm)
            gone(pe, "cg", NT - 1)
            for j in range(NT):
                g = take_slot("ca", j)
                for i in range(NT):
                    mm = pe.matmul(slot(g)[0:TILE, 0:HID], WA[:, i, j * TILE:j * TILE + TILE], G1[:, i, :],
                                   start=(i == 0), stop=(i == NT - 1))
                ready(mm)
            pe.wait_ge(ev("ca_in"), NT)
            for f in range(2):
                for n in range(2):
                    g = take_slot("cb", f, n)
                    ready(columns(g, n, P, [(G2[:, i, f * P:f * P + P], WA[:, i, :]) for i in range(NT)]))
            w = weights("cW2")[:, 0:2 * D].rearrange("p (k n) -> p k n", k=2)
            gone(pe, "cb", 1, 1)
            for i in range(NT):
                g = take_slot("co", i)
                for b in range(2):
                    for k in range(2):
                        mm = pe.matmul(slot(g)[0:TILE, 512 * b:512 * b + HALF], agT[:, k, i * TILE:i * TILE + TILE],
                                       w[:, k, b * HALF:b * HALF + HALF], start=(k == 0), stop=(k == 1))
                ready(mm)

            transposes("hin", hin, "ln_hin")
            pe.wait_ge(ev("T_hin_aff"), 1)
            token_major("vk", xT, ("vWk", 0), ("vWk", 1))
            token_major("vv", xT, ("vWv", 0), ("vWv", 1))
            pe.wait_ge(ev("kv_in"), 1)
            gone(pe, "vv", NT - 1)
            g = take_slot("vkv")
            for b in range(2):
                for i in range(NT):
                    mm = pe.matmul(slot(g)[0:TILE, 512 * b:512 * b + HALF], rk[:, i:i + 1].broadcast_to([TILE, TILE]),
                                   vK[:, i, b * HALF:b * HALF + HALF], start=(i == 0), stop=(i == NT - 1))
            ready(mm)
            token_major("vq", xT, ("vWq", 0), ("vWq", 1))
            transposes("at", H, "ln_at")
            pe.wait_ge(ev("T_at_aff"), 1)
            token_major("vo", xT, ("vWp", 0), ("vWp", 1))

            transposes("x4", H, "ln_x4")
            for o in range(2):
                for n in range(2):
                    take_slot("s1", o, n)
            for c in range(KT):
                for j in range(NCP):
                    if j % 8 == 0:
                        w = weights("kW1", c, j // 8)[:, 0:8 * HID].rearrange("p (j o) -> p j o", j=8)
                    m = c * NCP + j
                    pe.wait_ge(ev("basis"), m + 1)
                    for o in range(2):
                        for n in range(2):
                            g = packets["s1", o, n]
                            lo, wd_ = COLS[n]
                            for b in range(2):
                                mm = pe.matmul(slot(g)[:, 512 * b:512 * b + wd_], w[:, j % 8, o * P:o * P + P],
                                               kb[m % 3][:, lo + b * wd_:lo + b * wd_ + wd_],
                                               start=(m == 0), stop=(m == KT * NCP - 1), skip_group_check=True)
                            if m == KT * NCP - 1:
                                ready(mm)
                    if m < KT * NCP - 1:
                        mm.then_inc(ev("s1_mm"), 1)
            for i in range(NT):
                g = take_slot("s2", i)
                for hb in range(2):
                    m = 2 * i + hb
                    if i == 0:
                        pe.wait_ge(ev("kw2"), 32)
                    pe.wait_ge(ev("basis2"), m + 1)
                    bv = bb[m % 2].rearrange("p (j c n) -> p j c n", j=8, c=2)
                    for j in range(8):
                        for c in range(2):
                            for b in range(2):
                                mm = pe.matmul(slot(g)[0:TILE, 512 * b:512 * b + HALF], bv[:, j, c, :],
                                               w2v[:, c * NCP + hb * 8 + j, b * HALF:b * HALF + HALF],
                                               start=(hb == 0 and j == 0 and c == 0),
                                               stop=(hb == 1 and j == 7 and c == 1), skip_group_check=True)
                    if hb == 0:
                        mm.then_inc(ev("s2_mm"), 1)
                ready(mm)

        @block.scalar
        def _(act):
            own = Tally(act, act_step)

            def leave(g, dst, src, func=ACT.Copy, **kw):
                give(act.activation(dst, src, func, **kw), g)

            act.wait_ge(ev("flag"), 1)
            flag = act.value_load(flagi[0:1, 0:1], min_val=0, max_val=EDGES)

            def stage_block(par, b, tiles):
                act.wait_ge(ev("unstaged"), b + 1)
                act.wait_ge(ev("tiles_done"), (b + 1) * tiles + CREDIT)
                src = ps[0:TILE, 2 * par:2 * par + 2, :].rearrange("p s n -> p (s n)")[:, 0:NT * P]
                act.activation(stage[:, par].rearrange("p j k w -> p (j k w)"), src, ACT.Copy)\
                   .then_inc(ev("staged"), 1)

            with act.If(flag == 0):
                with act.Fori(0, NB // 2) as bp:
                    for par in range(2):
                        stage_block(par, bp * 2 + par, SPREAD)
            with act.Else():
                with act.Fori(0, NB // 2) as bp:
                    for par in range(2):
                        stage_block(par, bp * 2 + par, SPREAD * CHUNKS)

            norms = [0]

            def root():
                norms[0] += 1
                act.wait_ge(ev("var"), norms[0])
                act.activation(stdv, stdv, ACT.Sqrt).then_inc(ev("std"), 1)

            def transposed(s):
                for i in range(NT):
                    g = take(act, "T", s, i)
                    dst = xT[:, :, i * TILE:i * TILE + TILE].rearrange("p (b k) n -> p b k n", b=2)
                    leave(g, dst, banks(g, 375).rearrange("p b (k n) -> p b k n", k=3))

            def rows(dst, *keys):
                g = take(act, *keys[0])
                leave(g, dst[:, 0:1000].rearrange("p (b n) -> p b n", b=2), banks(g, 500)[0:TILE])
                g = take(act, *keys[1])
                leave(g, dst[:, 1000:1250], slot(g)[0:TILE, 0:250])

            root()
            transposed("xn")
            act.wait_ge(ev("spill"), 16)
            for i in range(NT):
                g = take(act, "mk", i)
                if i >= 2:
                    gone(act, "mk", i - 2)
                act.activation(tE[0:TILE, i % 2, 0:D].rearrange("p (b n) -> p b n", b=2),
                               banks(g, HALF)[0:TILE], ACT.Exp).then_inc(ev("exp_in"), 1)
            for i in range(NT):
                g = take(act, "mv", i)
                leave(g, H[:, i, :].rearrange("p (b n) -> p b n", b=2), banks(g, HALF)[0:TILE])
            for p in range(KT):
                for n in range(2):
                    g = take(act, "mq", p, n)
                    if p == 0:
                        gone(act, "mk", NT - 1)
                    else:
                        gone(act, "mq", p - 1, n)
                    w = COLS[n][1]
                    act.activation(tE[:, n, 0:2 * w].rearrange("p (b n) -> p b n", b=2), banks(g, w), ACT.Exp)\
                       .then_inc(ev("exp_in"), 1)

            for i in range(NT):
                g = take(act, "h1", i)
                leave(g, H97[:, i, :, 0:HC].rearrange("p (b h) c -> p b h c", b=2),
                      banks(g, HALF)[0:TILE].rearrange("p b (h c) -> p b h c", h=4))
            for h in range(HEADS):
                if h >= 2:
                    act.wait_ge(ev("smx"), h - 1)
                rows(srow[:, h % 2, :], ("srow", h, 0), ("srow", h, 1))

            act.wait_ge(ev("gD"), 1)
            act.wait_ge(ev("spill"), 32)

            def exponentials(n, i, h, d, reuse):
                if reuse is not None:
                    act.wait_ge(*reuse)
                if n >= 2:
                    act.wait_ge(ev("A_in"), n - 1)
                own.step(act.activation(AT[:, i, :], d[:, 0, :], ACT.Exp, bias=alS[:, i, h:h + 1]))
                act.activation(e2[:, n % 2, :], d[:, 1, :], ACT.Exp, bias=alS2[:, i, h:h + 1])\
                   .then_inc(ev("E_in"), 1)

            def shift_rows(m):
                if m >= 2:
                    act.wait_ge(ev("E_in"), (m - 1) * NT)
                for w in range(2):
                    rows(drow[:, m % 2, w, :], ("drow", m, w, 0), ("drow", m, w, 1))

            shift_rows(0)
            for h in range(HEADS):
                gone(act, "drow", h, 1, 1)
                for i in range(NT):
                    reuse = None
                    if h >= 1:
                        reuse = (packet_ready, packets["agg", h - 1] + 1) if i == NT - 1 else \
                            (ev("A_used"), (h - 1) * (NT - 1) + i + 1)
                    exponentials(h * NT + i, i, h, drow[:, h % 2], reuse)
                    if i == 4 and h + 1 < HEADS:
                        shift_rows(h + 1)
            for i in range(NT):
                act.wait_ge(ev("elu_b"), i + 1)
                if i >= 2:
                    act.wait_ge(ev("ln_x2"), i - 1)
                act.activation(aa_r[0:TILE, D * (i % 2):D * (i % 2) + D], O[:, i, :], ACT.Exp)\
                   .then_inc(ev("elu_e"), 1)
            transposed("x2")
            for i in range(NT):
                g = take(act, "h2", i)
                leave(g, H769[:, i, 0:D].rearrange("p (b n) -> p b n", b=2), banks(g, HALF)[0:TILE])
            rows(srow[:, 0, :], ("srow2", 0), ("srow2", 1))
            act.wait_ge(ev("gD"), 2)
            for w in range(2):
                rows(drow[:, 0, w, :], ("drow2", w, 0), ("drow2", w, 1))
            gone(act, "drow2", 1, 1)
            for i in range(NT):
                exponentials(HEADS * NT + i, i, 0, drow[:, 0], None)

            root()
            transposed("xf")
            act.wait_ge(ev("pshift"), 1)
            act.activation(pr, pr, ACT.Exp).then_inc(ev("pexp"), 1)
            for n in range(2):
                g = take(act, "cwT", n)
                own.step(act.activation(cwT[:, 625 * n:625 * n + 500], slot(g)[0:EXP, 0:500], ACT.Copy))
                leave(g, cwT[:, 625 * n + 500:625 * n + 625], slot(g)[0:EXP, 512:637])
            act.wait_ge(ev("cols"), 16 * 7)
            for e in range(EXP):
                for f in range(3):
                    for n in range(2):
                        g = take(act, "eh", e, f, n)
                        lo, w = COLS[n]
                        leave(g, hT[:, e % 2, f, lo:lo + 2 * w].rearrange("p (b n) -> p b n", b=2), banks(g, w),
                              ACT.Relu, bias=eb1[:, e, f:f + 1])

            root()
            transposed("x3")
            act.wait_ge(ev("deg_in"), 1)
            act.activation(dinv, dinv, ACT.Sqrt).then_inc(ev("deg_root"), 1)
            for n in range(2):
                g = take(act, "ad", n)
                lo, w = COLS[n]
                leave(g, uT[:, lo:lo + 2 * w].rearrange("p (b n) -> p b n", b=2), banks(g, w)[0:RANK],
                      ACT.Relu, bias=bd_c[0:RANK])
            for f in range(2):
                for n in range(2):
                    g = take(act, "cb", f, n)
                    lo, w = COLS[n]
                    leave(g, agT[:, f, lo:lo + 2 * w].rearrange("p (b n) -> p b n", b=2), banks(g, w))

            root()
            transposed("hin")
            for name, norm, dst in (("vk", rk, vK), ("vq", rq, H)):
                for i in range(NT):
                    g = take(act, name, i)
                    own.settle()
                    own.step(act.activation(sq.rearrange("p (b n) -> p b n", b=2), banks(g, HALF)[0:TILE],
                                            ACT.Square, accum_out=norm[:, i:i + 1]))
                    leave(g, dst[:, i, :].rearrange("p (b n) -> p b n", b=2), banks(g, HALF)[0:TILE])
                own.settle()
                act.activation(norm, norm, ACT.Sqrt).then_inc(ev("l2"), 1)
                if name == "vk":
                    g = take(act, "vkv")
                    leave(g, kvrow.rearrange("p (b n) -> p b n", b=2), banks(g, HALF)[0:TILE])
            root()
            transposed("at")

            root()
            transposed("x4")
            gone(act, "T", "x4", NT - 1)
            act.wait_ge(ev("consts"), 1)

            def distance(m):
                c, j = m // NCP, m % NCP
                if m >= 2:
                    act.wait_ge(ev("basis"), m - 1)
                act.activation(t1[m % 2], xT[:, c, :], ACT.Abs, bias=centre[:, j:j + 1], scale=1.0 / SPLINE_H)\
                   .then_inc(ev("dist"), 1)

            distance(0)
            for m in range(KT * NCP):
                if m + 1 < KT * NCP:
                    distance(m + 1)
                act.wait_ge(ev("pieces2"), m + 1)
                if m >= 3:
                    act.wait_ge(ev("s1_mm"), m - 2)
                own.step(act.activation(kb[m % 3], kns[m % 2], ACT.Square))
                act.activation(kq2[m % 2], t1[m % 2], ACT.Square).then_inc(ev("squares"), 1)
            for o in range(2):
                for n in range(2):
                    g = take(act, "s1", o, n)
                    lo, w = COLS[n]
                    leave(g, h1T[:, o, lo:lo + 2 * w].rearrange("p (b n) -> p b n", b=2), banks(g, w),
                          ACT.Copy, scale=-1.0 / 6.0)
            gone(act, "s1", 1, 1)
            for m in range(2 * NT):
                i, hb = m // 2, m % 2
                if m >= 1:
                    act.wait_ge(ev("basis2"), m)
                for j in range(8):
                    ins = act.activation(b2a.rearrange("p (j c n) -> p j c n", j=8, c=2)[:, j],
                                         h1T[:, :, i * TILE:i * TILE + TILE], ACT.Abs,
                                         bias=centre[:, 8 * hb + j:8 * hb + j + 1], scale=1.0 / SPLINE_H)
                ins.then_inc(ev("dist2"), 1)
                act.wait_ge(ev("pieces3"), m + 1)
                if m >= 2:
                    if hb == 0:
                        act.wait_ge(ev("s2_mm"), i)
                    else:
                        act.wait_ge(packet_ready, packets["s2", i - 1] + 1)
                own.step(act.activation(b2s2, b2ns, ACT.Square))
                act.activation(bb[m % 2], b2a, ACT.Square).then_inc(ev("squares2"), 1)

        @block.vector
        def _(dve):
            own = Tally(dve, dve_step)

            def chain(ins):
                own.step(ins)
                own.settle()

            dve.wait_ge(ev("edges"), 16 * 9)
            for a in range(2):
                own.step(dve.tensor_copy(rawf[:, a], raw[:, a].bitcast(I32)))
            dve.tensor_copy(rawf[:, 2], raw[:, 2]).then_inc(ev("edges_f"), 1)
            own.step(dve.memset(src_c[:, 0:PRE], -1.0))
            own.step(dve.memset(dst_c[:, 0:PRE], -1.0))
            own.step(dve.memset(w_f[:, 0:PRE], 0.0))
            dve.wait_ge(ev("edges_t"), 3)
            for a, c in enumerate((src_c, dst_c, w_f)):
                own.step(dve.tensor_copy(c[:, PRE:ECOLS], ps[:, a, 0:3 * P]))
            own.settle()
            chain(dve.tensor_copy(w_c[0], w_f))
            chain(dve.tensor_tensor(w_f, w_f, w_c[0], ALU.subtract))
            chain(dve.tensor_copy(w_c[1], w_f))
            chain(dve.tensor_tensor(w_f, w_f, w_c[1], ALU.subtract))
            chain(dve.tensor_copy(w_c[2], w_f))
            dve.wait_ge(ev("consts"), 1)
            lo, hi = PRE, PRE + ET
            chain(dve.tensor_tensor(w_f[:, lo:hi], dst_c[:, lo:hi], hi_row[:, lo:hi], ALU.subtract))
            chain(dve.tensor_scalar(viol[:, lo:hi], w_f[:, lo:hi], 0.0, None, ALU.is_ge))
            chain(dve.tensor_scalar(hi_row[:, lo:hi], w_f[:, lo:hi], -2.0 * WIN, None, ALU.is_lt))
            chain(dve.tensor_tensor(viol[:, lo:hi], viol[:, lo:hi], hi_row[:, lo:hi], ALU.add))
            chain(dve.memset(viol[64:P, hi - 1:hi], 0.0))
            dve.tensor_reduce(flagf[:, 0:1], viol[:, lo:hi], AXX, ALU.add).then_inc(ev("viol"), 1)
            dve.wait_ge(ev("flag_sum"), 1)
            dve.tensor_copy(flagi[0:1, 0:1], ps[0:1, 3, 0:1]).then_inc(ev("flag"), 1)
            dve.wait_ge(ev("flag"), 1)
            flag = dve.value_load(flagi[0:1, 0:1], min_val=0, max_val=EDGES)

            def destinations(par, col, count, free, b):
                dve.wait_ge(ev("next_block"), b + 1)
                dve.wait_ge(ev("tiles_done"), free)
                dve.tensor_tensor(oh_dst[:, par, :, 0, :],
                                  dst_c[:, bass.ds(col, SPREAD)].unsqueeze(2).broadcast_to([P, SPREAD, WIN]),
                                  iota_b.unsqueeze(1).broadcast_to([P, SPREAD, WIN]), ALU.is_equal)\
                   .then_inc(ev("dst_plain"), 1)
                dve.wait_ge(ev("dst_plain"), count + 1)
                for k in range(3):
                    ins = dve.tensor_tensor(oh_dst[:, par, :, 1 + k, :], oh_dst[:, par, :, 0, :],
                                            w_c[k][:, bass.ds(col, SPREAD)].unsqueeze(2).broadcast_to([P, SPREAD, WIN]),
                                            ALU.mult)
                ins.then_inc(ev("dst_hot"), 1)

            def sources(col, tile0):
                for u in range(SPREAD):
                    dve.wait_ge(ev("tiles_done"), tile0 + (u + 1 - RING + CREDIT))
                    dve.tensor_scalar(oh_src[:, u % RING, :], iota_src, src_c[:, bass.ds(col + u, 1)], None,
                                      ALU.is_equal).then_inc(ev("src_hot"), 1)

            def next_block():
                dve.tensor_scalar(iota_b, iota_b, float(WIN), None, ALU.add).then_inc(ev("next_block"), 1)

            with dve.If(flag == 0):
                with dve.Fori(0, NB // 2) as bp:
                    for par in range(2):
                        b = bp * 2 + par
                        destinations(par, b * TB, b, b * SPREAD - SPREAD + CREDIT, b)
                        next_block()
                        sources(b * TB, b * SPREAD)
            with dve.Else():
                with dve.Fori(0, NB // 2) as bp:
                    for par in range(2):
                        b = bp * 2 + par
                        with dve.Fori(0, CHUNKS) as ch:
                            n = b * CHUNKS + ch
                            destinations(par, ch * SPREAD + PRE, n, n * SPREAD + CREDIT, b)
                            sources(ch * SPREAD + PRE, n * SPREAD)
                        next_block()

            norms = [0]

            def layer_norm(s, src, dst):
                for i in range(NT):
                    for c in range(2):
                        own.step(dve.bn_stats(st[:, i, c, :], src[:, i, c * HALF:c * HALF + HALF]))
                own.settle()
                for i in range(NT):
                    own.step(dve.bn_aggr(mv[:, i, :], st[:, i].rearrange("p c s -> p (c s)")))
                own.settle()
                dve.tensor_scalar(stdv, mv[:, :, 1], LN_EPS, None, ALU.add).then_inc(ev("var"), 1)
                norms[0] += 1
                dve.wait_ge(ev("std"), norms[0])
                chain(dve.reciprocal(rstd, stdv))
                for i in range(NT):
                    dve.tensor_scalar(dst[:, i, :], src[:, i, :], mv[:, i, 0:1], rstd[:, i:i + 1],
                                      ALU.subtract, ALU.mult).then_inc(ev("ln_" + s), 1)

            def two(a):
                return a.rearrange("p (b n) -> p b n", b=2)

            def add_packet(i, *key, scalar=1.0):
                g = take(dve, *key)
                give(dve.scalar_tensor_tensor(out=two(acc[:, i, :]), in0=banks(g, HALF)[0:TILE], scalar=scalar,
                                              in1=two(acc[:, i, :]), op0=ALU.mult, op1=ALU.add), g)

            rowbs = [0]

            def bias_row():
                rowbs[0] += 1
                dve.wait_ge(ev("rowb"), 16 * rowbs[0])

            def add_bias_row():
                bias_row()
                dve.tensor_tensor(acc, acc, rowb[0:TILE].unsqueeze(1).broadcast_to([TILE, NT, D]), ALU.add)\
                   .then_inc(ev("rowb_used"), 1)
                dve.wait_ge(ev("rowb_used"), rowbs[0])

            dve.wait_ge(ev("x"), 16)
            dve.wait_ge(ev("adj_all"), 1)
            layer_norm("xn", acc, H)
            exps = [0]

            def feature_map(g, e, dst):
                exps[0] += 1
                dve.wait_ge(ev("exp_in"), exps[0])
                chain(dve.tensor_scalar(e, e, 1.0, None, ALU.min))
                w = e.shape[-1] // 2
                give(dve.scalar_tensor_tensor(out=two(dst), in0=banks(g, w)[0:e.shape[0]], scalar=0.0, in1=two(e),
                                              op0=ALU.max, op1=ALU.add), g)

            dve.wait_ge(ev("spill"), 16)
            own.step(dve.memset(Pbd, 0.0))
            own.step(dve.memset(Kbd, 0.0))
            for i in range(NT):
                g = take(dve, "mk", i)
                feature_map(g, tE[0:TILE, i % 2, 0:D], mK[:, i, :])
            own.settle()
            for q in range(2):
                g = take(dve, "mP", q)
                for p in range(4 * q, min(4 * q + 4, KT)):
                    for hd in range(2):
                        rows_, o = slice(FD * hd, FD * hd + FD), 256 * (p % 4) + FD * hd
                        own.step(dve.tensor_copy(Pbd[rows_, p, FD * hd:FD * hd + FD], slot(g)[rows_, o:o + FD]))
                        ins = dve.tensor_copy(Kbd[rows_, p, FD * hd:FD * hd + FD], slot(g)[rows_, o + P:o + P + FD])
                        if not (hd == 1 and p == min(4 * q + 3, KT - 1)):
                            own.step(ins)
                give(ins, g)
            own.settle()
            gone(dve, "mP", 1)
            dve.tensor_copy(rz, stdv).then_inc(ev("P_in"), 1)
            for p in range(KT):
                for n in range(2):
                    lo, w = COLS[n]
                    g = take(dve, "mq", p, n)
                    feature_map(g, tE[:, n, 0:2 * w], qT[:, p % 2, lo:lo + 2 * w])
                for n in range(2):
                    lo, w = COLS[n]
                    gy, gz_ = packets["my", p, n], take(dve, "mz", p, n)
                    r = ct_r[:, 6400 + 640 * n:6400 + 640 * n + 2 * w]
                    if p >= 1:
                        emptied(dve, "my", p - 1, n)
                    give(dve.tensor_scalar(two(r), banks(gz_, w), 1e-6, None, ALU.add), gz_)
                    gone(dve, "mq", p, n)
                    dve.wait_ge(slot_free[gz_ % 4], gz_ // 4 + 1)
                    chain(dve.reciprocal(r, r))
                    give(dve.tensor_tensor(two(yT[:, p, lo:lo + 2 * w]), banks(gy, w), two(r), ALU.mult), gy)
            add_bias_row()
            add_bias_row()
            for i in range(NT):
                add_packet(i, "mo", i)
            gone(dve, "mo", NT - 1)
            dve.tensor_copy(rz, stdv).then_inc(ev("mo_done"), 1)

            attn = [0]

            def logits(hv, nh):
                dve.wait_ge(ev("arow"), 32 * (attn[0] + 1))
                for i in range(NT):
                    for w in range(2):
                        own.step(dve.tensor_tensor(prod[:, w, :].rearrange("p (h c) -> p h c", h=nh), hv(i),
                                                   arow[:, w, :].rearrange("p (h c) -> p h c", h=nh), ALU.mult))
                    own.settle()
                    for w, al in enumerate((alS, alD)):
                        own.step(dve.tensor_reduce(al[:, i, 0:nh], prod[:, w, :].rearrange("p (h c) -> p h c", h=nh),
                                                   AXX, ALU.add))
                    own.settle()
                dve.tensor_scalar(alS2[:, :, 0:nh], alS[:, :, 0:nh], SPAN, None, ALU.mult).then_inc(ev("al"), 1)

            def shifts(nh):
                own.settle()
                z, m = gz[:, :, 0:nh], smax[:, :, 0:nh]
                d = alD[:, :, 0:nh]
                chain(dve.tensor_tensor(z, m, d, ALU.add))
                chain(dve.scalar_tensor_tensor(out=m, in0=z, scalar=SPAN, in1=z, op0=ALU.mult, op1=ALU.max))
                own.step(dve.tensor_tensor(gD1[:, :, 0:nh], d, m, ALU.subtract))
                own.settle()
                dve.scalar_tensor_tensor(out=gD2[:, :, 0:nh], in0=d, scalar=SPAN, in1=m, op0=ALU.mult,
                                         op1=ALU.subtract).then_inc(ev("gD"), 1)
                attn[0] += 1

            def segment_max(neg, row, j, h):
                chain(dve.tensor_tensor_reduce(out=dummy, in0=neg[:, j, :], in1=row, scale=1.0, scalar=-3.0e38,
                                               op0=ALU.add, op1=ALU.max, accum_out=smax[:, j, h:h + 1]))

            def weigh(n, i):
                dve.wait_ge(ev("E_in"), n + 1)
                chain(dve.tensor_tensor(AT[:, i, :], AT[:, i, :], e2[:, n % 2, :], ALU.max))
                dve.scalar_tensor_tensor(out=AT[:, i, :], in0=AT[:, i, :], scalar=1.0, in1=CT[:, i, 0:NODES],
                                         op0=ALU.min, op1=ALU.mult).then_inc(ev("A_in"), 1)

            take(dve, "h1", 0)
            own.step(dve.memset(H97[:, :, :, HC:HC + 1], 1.0))
            gone(dve, "h1", NT - 1)
            logits(lambda i: H97[:, i, :, 0:HC], HEADS)
            for j in range(NT):
                for q in range(3):
                    g = take(dve, "neg", j, q)
                    n = 4 if q < 2 else 2
                    src = slot(g)[0:TILE, 0:252].bitcast(FP16).rearrange("p (i n) -> p i n", i=4)[:, 0:n, 0:TILE]
                    dst = negA[:, j, 500 * q:500 * q + TILE * n].rearrange("p (i n) -> p i n", i=n)
                    give(dve.tensor_scalar(dst, src, 0.0, FAR, ALU.is_equal, ALU.mult), g)
            gone(dve, "neg", NT - 1, 2)
            dve.tensor_copy(rz, stdv).then_inc(ev("neg_done"), 1)
            for h in range(HEADS):
                gone(dve, "srow", h, 1)
                for j in range(NT):
                    segment_max(negA, srow[:, h % 2, :], j, h)
                own.settle()
                dve.tensor_copy(rz, stdv).then_inc(ev("smx"), 1)
            shifts(HEADS)

            def aggregate(h):
                g = take(dve, "agg", h)
                v = banks(g, 485)[0:TILE].rearrange("p b (j c) -> p b j c", c=97)
                r = rz.rearrange("p (b j) -> p b j", b=2)
                chain(dve.tensor_scalar(r.unsqueeze(3), v[:, :, :, HC:HC + 1], 1e-16, None, ALU.add))
                chain(dve.reciprocal(rz, rz))
                for b in range(2):
                    ins = dve.tensor_tensor(O[:, 5 * b:5 * b + 5, h * HC:h * HC + HC], v[:, b, :, 0:HC],
                                            r[:, b].unsqueeze(2).broadcast_to([TILE, 5, HC]), ALU.mult)
                    if b == 0:
                        own.step(ins)
                give(ins, g)

            for h in range(HEADS):
                for i in range(NT):
                    weigh(h * NT + i, i)
                    if h >= 1 and i == 1:
                        aggregate(h - 1)
            aggregate(HEADS - 1)
            bias_row()
            gone(dve, "agg", HEADS - 1)
            own.settle()
            for i in range(NT):
                dve.tensor_tensor(O[:, i, :], O[:, i, :], rowb[0:TILE], ALU.add).then_inc(ev("elu_b"), 1)
            dve.wait_ge(ev("elu_b"), NT)
            dve.tensor_copy(rz, stdv).then_inc(ev("rowb_used"), 1)
            for i in range(NT):
                dve.wait_ge(ev("elu_e"), i + 1)
                chain(dve.tensor_scalar(O[:, i, :], O[:, i, :], 0.0, -1.0, ALU.max, ALU.add))
                dve.scalar_tensor_tensor(out=O[:, i, :], in0=aa_r[0:TILE, D * (i % 2):D * (i % 2) + D], scalar=1.0,
                                         in1=O[:, i, :], op0=ALU.min, op1=ALU.add).then_inc(ev("ln_x2"), 1)
            take(dve, "h2", 0)
            own.step(dve.memset(H769[:, :, D:D + 1], 1.0))
            gone(dve, "h2", NT - 1)
            logits(lambda i: H769[:, i, 0:D].unsqueeze(1), 1)
            dve.wait_ge(ev("neg_back"), 16)
            gone(dve, "srow2", 1)
            for j in range(NT):
                segment_max(negX, srow[:, 0, :], j, 0)
            shifts(1)
            for i in range(NT):
                weigh(HEADS * NT + i, i)
            for j in range(NT):
                g = take(dve, "agg2", j)
                z = slot(g)[0:TILE, 512 + 383:512 + 384]
                chain(dve.tensor_scalar(rz[:, j:j + 1], z, 1e-16, None, ALU.add))
                chain(dve.reciprocal(rz[:, j:j + 1], rz[:, j:j + 1]))
                own.step(dve.scalar_tensor_tensor(out=acc[:, j, 0:385], in0=slot(g)[0:TILE, 0:385],
                                                  scalar=rz[:, j:j + 1], in1=acc[:, j, 0:385],
                                                  op0=ALU.mult, op1=ALU.add))
                give(dve.scalar_tensor_tensor(out=acc[:, j, 385:D], in0=slot(g)[0:TILE, 512:512 + 383],
                                              scalar=rz[:, j:j + 1], in1=acc[:, j, 385:D],
                                              op0=ALU.mult, op1=ALU.add), g)
            gone(dve, "agg2", NT - 1)
            own.settle()

            layer_norm("xf", acc, H)
            g = take(dve, "logit")
            give(dve.tensor_copy(pr, slot(g)[0:TILE, 0:80].rearrange("p (t e) -> p t e", t=NT)), g)
            gone(dve, "logit")
            chain(dve.tensor_reduce(rsum, pr, AXX, ALU.max))
            dve.tensor_tensor(pr, pr, rsum.unsqueeze(2).broadcast_to([TILE, NT, EXP]), ALU.subtract)\
               .then_inc(ev("pshift"), 1)
            dve.wait_ge(ev("pexp"), 1)
            chain(dve.tensor_reduce(rsum, pr, AXX, ALU.add))
            chain(dve.reciprocal(rsum, rsum))
            chain(dve.tensor_tensor(pr, pr, rsum.unsqueeze(2).broadcast_to([TILE, NT, EXP]), ALU.mult))
            chain(dve.memset(rank, 0.0))
            for e in range(EXP):
                for lo, hi, op in ((0, e, ALU.is_gt), (e + 1, EXP, ALU.is_ge)):
                    if lo < hi:
                        o = cmpb[:, :, lo:hi]
                        chain(dve.tensor_tensor(o, pr[:, :, e:e + 1].broadcast_to([TILE, NT, hi - lo]),
                                                pr[:, :, lo:hi], op))
                        chain(dve.tensor_tensor(rank[:, :, lo:hi], rank[:, :, lo:hi], o, ALU.add))
            chain(dve.scalar_tensor_tensor(out=cw, in0=rank, scalar=1.5, in1=pr, op0=ALU.is_lt, op1=ALU.mult))
            chain(dve.tensor_reduce(rsum, cw, AXX, ALU.add))
            chain(dve.reciprocal(rsum, rsum))
            dve.tensor_tensor(cw, cw, rsum.unsqueeze(2).broadcast_to([TILE, NT, EXP]), ALU.mult)\
               .then_inc(ev("cw"), 1)
            dve.wait_ge(ev("cw"), 1)
            for i in range(NT):
                add_packet(i, "eb", i)
            gone(dve, "eb", NT - 1)
            for e in range(EXP):
                for i in range(NT):
                    add_packet(i, "eo", e, i, scalar=cw[:, i, e:e + 1])
                gone(dve, "eo", e, NT - 1)

            layer_norm("x3", acc, H)
            g = take(dve, "deg")
            give(dve.tensor_copy(dinv, slot(g)[0:TILE, 0:NT]), g)
            gone(dve, "deg")
            dve.tensor_copy(rz, dinv).then_inc(ev("deg_in"), 1)
            dve.wait_ge(ev("deg_root"), 1)
            chain(dve.reciprocal(dinv, dinv))
            dve.wait_ge(ev("cols"), 16 * 7)
            for k in range(KT):
                for n in range(2):
                    g = take(dve, "ah", k, n)
                    lo, w = COLS[n]
                    give(dve.scalar_tensor_tensor(out=two(haT[:, k, lo:lo + 2 * w]), in0=banks(g, w),
                                                  scalar=bu_c[:, k:k + 1], in1=two(xT[:, k, lo:lo + 2 * w]),
                                                  op0=ALU.add, op1=ALU.add), g)
            for i in range(NT):
                g = take(dve, "cg", i)
                give(dve.tensor_scalar(G1[:, i, :], slot(g)[0:TILE, 0:HID], dinv[:, i:i + 1], None, ALU.mult), g)
            bias_row()
            for j in range(NT):
                g = take(dve, "ca", j)
                give(dve.scalar_tensor_tensor(out=gtmp[:, j, :], in0=slot(g)[0:TILE, 0:HID], scalar=dinv[:, j:j + 1],
                                              in1=rowb[0:TILE, 0:HID], op0=ALU.mult, op1=ALU.add), g)
                dve.wait_ge(slot_free[g % 4], g // 4 + 1)
                dve.tensor_scalar(G2[:, j, :], gtmp[:, j, :], 0.0, dinv[:, j:j + 1], ALU.max, ALU.mult)\
                   .then_inc(ev("ca_in"), 1)
            dve.wait_ge(ev("ca_in"), NT)
            dve.tensor_copy(rz, dinv).then_inc(ev("rowb_used"), 1)
            add_bias_row()
            for i in range(NT):
                add_packet(i, "co", i, scalar=dinv[:, i:i + 1])

            layer_norm("hin", H, hin)

            def affine(s, w):
                gone(dve, "T", s, NT - 1)
                for k in range(KT):
                    ins = dve.tensor_scalar(xT[:, k, :], xT[:, k, :], gb_c[:, w, k:k + 1], gb_c[:, w + 1, k:k + 1],
                                            ALU.mult, ALU.add)
                ins.then_inc(ev("T_" + s + "_aff"), 1)

            affine("hin", 0)
            for i in range(NT):
                g = take(dve, "vv", i)
                if i == 0:
                    gone(dve, "vk", NT - 1)
                give(dve.tensor_tensor(two(vK[:, i, :]), banks(g, HALF)[0:TILE], two(vK[:, i, :]), ALU.mult), g)
            dve.wait_ge(ev("l2"), 1)
            chain(dve.tensor_scalar(rk, rk, 1e-12, None, ALU.max))
            dve.reciprocal(rk, rk).then_inc(ev("kv_in"), 1)
            dve.wait_ge(ev("l2"), 2)
            chain(dve.tensor_scalar(rq, rq, 1e-12, None, ALU.max))
            chain(dve.reciprocal(rq, rq))
            gone(dve, "vq", NT - 1)
            for i in range(NT):
                own.step(dve.scalar_tensor_tensor(out=H[:, i, :], in0=H[:, i, :], scalar=rq[:, i:i + 1], in1=kvrow,
                                                  op0=ALU.mult, op1=ALU.mult))
            own.settle()
            layer_norm("at", H, H)
            affine("at", 2)
            for i in range(NT):
                add_packet(i, "vo", i)
            gone(dve, "vo", NT - 1)

            layer_norm("x4", acc, H)

            def parts(m):
                dve.wait_ge(ev("dist"), m + 1)
                if m == 0:
                    take(dve, "T", "x4", NT - 1)
                own.step(dve.tensor_scalar(kns[m % 2], t1[m % 2], 2.0, -2.0, ALU.min, ALU.add))
                own.settle()
                dve.tensor_scalar(t1[m % 2], t1[m % 2], 1.0, -1.0, ALU.min, ALU.add).then_inc(ev("pieces2"), 1)

            parts(0)
            for m in range(KT * NCP):
                if m + 1 < KT * NCP:
                    parts(m + 1)
                dve.wait_ge(ev("squares"), m + 1)
                own.step(dve.tensor_tensor(kb[m % 3], kb[m % 3], kns[m % 2], ALU.mult))
                chain(dve.scalar_tensor_tensor(out=kq2[m % 2], in0=kq2[m % 2], scalar=-4.0, in1=t1[m % 2],
                                               op0=ALU.mult, op1=ALU.mult))
                dve.tensor_tensor(kb[m % 3], kb[m % 3], kq2[m % 2], ALU.add).then_inc(ev("basis"), 1)
            for m in range(2 * NT):
                i = m // 2
                dve.wait_ge(ev("dist2"), m + 1)
                chain(dve.tensor_scalar(b2ns, b2a, 2.0, -2.0, ALU.min, ALU.add))
                dve.tensor_scalar(b2a, b2a, 1.0, -1.0, ALU.min, ALU.add).then_inc(ev("pieces3"), 1)
                if m % 2 == 0 and m >= 2:
                    add_packet(i - 1, "s2", i - 1, scalar=-1.0 / 6.0)
                    dve.wait_ge(slot_free[packets["s2", i - 1] % 4], packets["s2", i - 1] // 4 + 1)
                    dve.tensor_copy(rz, dinv).then_inc(ev("final"), 1)
                dve.wait_ge(ev("squares2"), m + 1)
                own.step(dve.tensor_tensor(b2s2, b2s2, b2ns, ALU.mult))
                chain(dve.scalar_tensor_tensor(out=bb[m % 2], in0=bb[m % 2], scalar=-4.0, in1=b2a,
                                               op0=ALU.mult, op1=ALU.mult))
                dve.tensor_tensor(bb[m % 2], bb[m % 2], b2s2, ALU.add).then_inc(ev("basis2"), 1)
            add_packet(NT - 1, "s2", NT - 1, scalar=-1.0 / 6.0)
            g = packets["s2", NT - 1]
            dve.wait_ge(slot_free[g % 4], g // 4 + 1)
            dve.tensor_copy(rz, dinv).then_inc(ev("final"), 1)


_INS = ['x', 'src', 'dst', 'edge_weight', 'L0_gnn_W1', 'L0_gnn_a_src1', 'L0_gnn_a_dst1', 'L0_gnn_b1', 'L0_gnn_W2',
        'L0_gnn_a_src2', 'L0_gnn_a_dst2', 'L0_gnn_b2', 'L0_mix_b_proj', 'L0_ffn_Wg', 'L0_ffn_W1', 'L0_ffn_b1',
        'L0_ffn_W2', 'L0_ffn_b2', 'L1_gnn_Wd', 'L1_gnn_bd', 'L1_gnn_Wu', 'L1_gnn_bu', 'L1_gnn_W1', 'L1_gnn_b1',
        'L1_gnn_W2', 'L1_gnn_b2', 'L1_mix_w_qkv', 'L1_mix_w_proj', 'L1_mix_ln_in_g', 'L1_mix_ln_in_b',
        'L1_mix_ln_out_g', 'L1_mix_ln_out_b']
_TURNED = {'mixT': ('L0_mix_W_qkv', (1, 0)), 'projT': ('L0_mix_W_proj', (1, 0)),
           'kw1': ('L1_ffn_w1', (2, 1, 0)), 'kw2': ('L1_ffn_w2', (2, 1, 0))}


def kernel(**inputs):
    import numpy as _np
    import concourse.bacc as _bacc
    from concourse import mybir as _mybir
    from concourse.bass_utils import run_bass_kernel_spmd as _run

    nc = _bacc.Bacc("TRN2", target_bir_lowering=False, num_devices=1)
    arrays, A = {}, {}
    laid = {n: _np.ascontiguousarray(inputs[n]) for n in _INS}
    for n, (of, axes) in _TURNED.items():
        laid[n] = _np.ascontiguousarray(_np.transpose(_np.asarray(inputs[of]), axes))
    for n, a in laid.items():
        arrays[f"in_{n}_dram"] = a
        A[n] = nc.dram_tensor(f"in_{n}_dram", a.shape, _mybir.dt.from_np(a.dtype), kind="ExternalInput").ap()
    A["spill_w"] = nc.dram_tensor("spill_w", (TILE, NT, NODES_P), F32).ap()
    A["spill_n"] = nc.dram_tensor("spill_n", (TILE, NT, NODES), BF16).ap()
    out = nc.dram_tensor("out_0_dram", (NODES, D), F32, kind="ExternalOutput").ap()
    build(nc, A, out)
    r = _run(nc, [arrays], core_ids=[0])
    return r.results[0]["out_0_dram"]
```
